# Optimizing a Trainium2 kernel written in Bass

```python
import numpy as np
import jax
import jax.numpy as jnp

def _softmax(x, axis=-1):
    return jax.nn.softmax(x, axis=axis)

def _gelu(x):
    return jax.nn.gelu(x, approximate=True)

def _silu(x):
    return jax.nn.silu(x)

def _sigmoid(x):
    return jax.nn.sigmoid(x)

def _layernorm(x, axis=-1, eps=1e-05):
    m = jnp.mean(x, axis=axis, keepdims=True)
    v = jnp.var(x, axis=axis, keepdims=True)
    return (x - m) / jnp.sqrt(v + eps)

def _scatter_add(tgt, idx, src, axis=0):
    return tgt.at[idx].add(src)

def _segment_sum(src, seg, n):
    return jax.ops.segment_sum(src, seg, n)
kernel_name = 'mk_xattn_ffn_d1_seqx_r8_fec650'

def setup_inputs(seed: int=0):
    np.random.seed(seed)
    _w = jnp.asarray

    def _rec_inputs():
        import jax
        import jax.numpy as jnp
        _rk = jax.random.key(seed)
        x = 0.0002417 + 0.9998 * jax.random.normal(jax.random.fold_in(_rk, 1), (4, 256, 128), jnp.float32)
        _lenS = 256 - jax.random.randint(jax.random.fold_in(_rk, 7), (4,), 0, max(1, 256 // 4) + 1, jnp.int32)
        _lenS2 = 1601 - jax.random.randint(jax.random.fold_in(_rk, 8), (4,), 0, max(1, 1601 // 4) + 1, jnp.int32)
        _ctx_1024P = jax.random.normal(jax.random.fold_in(_rk, 11), (4, 16, 128), jnp.float32)
        _ctx_1024c = jax.random.dirichlet(jax.random.fold_in(_rk, 511), 0.3 * jnp.ones((16,), jnp.float32), (4, 1601))
        _ctx_1024t = jnp.einsum('bsk,bkd->bsd', _ctx_1024c, _ctx_1024P)
        _ctx_1024t = _ctx_1024t * jax.lax.rsqrt(jnp.mean(jnp.square(_ctx_1024t)) + 1e-12) * 0.953939
        ctx_1024 = 7.22013e-05 + 1.00017 * (_ctx_1024t + 0.3 * jax.random.normal(jax.random.fold_in(_rk, 611), (4, 1601, 128), jnp.float32))
        return (x, ctx_1024)
    x, ctx_1024 = _rec_inputs()

    def _L0_xattn_setup():
        import jax, jax.numpy as jnp
        import numpy as np
        D_MODEL = 128
        B, S = (4, 256)
        key = jax.random.key(seed)
        ks = jax.random.split(key, 10)
        s = 1.0 / np.sqrt(D_MODEL)
        return {'k': jax.random.normal(ks[0], (B, S, D_MODEL), jnp.float32), 'v': jax.random.normal(ks[1], (B, S, D_MODEL), jnp.float32), 'q': jax.random.normal(ks[2], (B, S, D_MODEL), jnp.float32), 'Wk': jax.random.normal(ks[3], (D_MODEL, D_MODEL), jnp.float32) * s, 'Wv': jax.random.normal(ks[4], (D_MODEL, D_MODEL), jnp.float32) * s, 'bv': jnp.zeros((D_MODEL,), jnp.float32), 'Wq': jax.random.normal(ks[5], (D_MODEL, D_MODEL), jnp.float32) * s, 'bq': jnp.zeros((D_MODEL,), jnp.float32), 'Wo': jax.random.normal(ks[6], (D_MODEL, D_MODEL), jnp.float32) * s, 'bo': jnp.zeros((D_MODEL,), jnp.float32)}
    _L0_xattn_all = _L0_xattn_setup()
    _L0_xattn_in = {k: v for k, v in _L0_xattn_all.items() if k in ('Wk', 'Wv', 'bv', 'Wq', 'bq', 'Wo', 'bo')}
    del _L0_xattn_all

    def _L0_ffn_setup():
        import jax, jax.numpy as jnp
        import numpy as np
        B, S, D, F, E, K = (4, 256, 128, 512, 4, 2)
        key = jax.random.key(seed)
        k = jax.random.split(key, 6)
        x = jax.random.normal(k[0], (B, S, D), jnp.float32)
        router_w = jax.random.normal(k[1], (D, E), jnp.float32) * D ** (-0.5)
        router_b = jnp.zeros((E,), jnp.float32)
        w1 = jax.random.normal(k[2], (E, D, F), jnp.float32) * 0.02
        w3 = jax.random.normal(k[3], (E, D, F), jnp.float32) * 0.02
        w2 = jax.random.normal(k[4], (E, F, D), jnp.float32) * 0.02
        return {'x': x, 'router_w': router_w, 'router_b': router_b, 'w1': w1, 'w3': w3, 'w2': w2}
    _L0_ffn_all = _L0_ffn_setup()
    _L0_ffn_in = {k: v for k, v in _L0_ffn_all.items() if k in ('router_w', 'router_b', 'w1', 'w3', 'w2')}
    del _L0_ffn_all
    return {'x': x, 'ctx_1024': ctx_1024, 'L0_xattn_Wk': _L0_xattn_in['Wk'], 'L0_xattn_Wv': _L0_xattn_in['Wv'], 'L0_xattn_bv': _L0_xattn_in['bv'], 'L0_xattn_Wq': _L0_xattn_in['Wq'], 'L0_xattn_bq': _L0_xattn_in['bq'], 'L0_xattn_Wo': _L0_xattn_in['Wo'], 'L0_xattn_bo': _L0_xattn_in['bo'], 'L0_ffn_router_w': _L0_ffn_in['router_w'], 'L0_ffn_router_b': _L0_ffn_in['router_b'], 'L0_ffn_w1': _L0_ffn_in['w1'], 'L0_ffn_w3': _L0_ffn_in['w3'], 'L0_ffn_w2': _L0_ffn_in['w2']}

def reference(x, ctx_1024, L0_xattn_Wk, L0_xattn_Wv, L0_xattn_bv, L0_xattn_Wq, L0_xattn_bq, L0_xattn_Wo, L0_xattn_bo, L0_ffn_router_w, L0_ffn_router_b, L0_ffn_w1, L0_ffn_w3, L0_ffn_w2):
    import jax
    import jax.numpy as jnp

    def _L0_xattn_ref(k, v, q, Wk, Wv, bv, Wq, bq, Wo, bo):
        import jax, jax.numpy as jnp
        import numpy as np
        D_MODEL = 128
        B, S = (4, 256)
        kp = jnp.einsum('bsd,ed->bse', k, Wk)
        vp = jnp.einsum('bsd,ed->bse', v, Wv) + bv
        qp = jnp.einsum('bsd,ed->bse', q, Wq) + bq
        scale = 1.0 / jnp.sqrt(jnp.float32(kp.shape[-1]))
        scores = jnp.einsum('bqd,bkd->bqk', qp, kp) * scale
        probs = jax.nn.softmax(scores, axis=-1)
        ctx = jnp.einsum('bqk,bkd->bqd', probs, vp)
        return jnp.einsum('bqd,ed->bqe', ctx, Wo) + bo

    def _L0_ffn_ref(x, router_w, router_b, w1, w3, w2):
        import jax, jax.numpy as jnp
        import numpy as np
        B, S, D, F, E, K = (4, 256, 128, 512, 4, 2)
        b, s, d = x.shape
        T = b * s
        e = router_w.shape[1]
        xf = x.reshape(T, d)
        logits = xf @ router_w + router_b
        probs = jax.nn.softmax(logits, axis=-1)
        top_p, top_i = jax.lax.top_k(probs, K)
        top_p = top_p / jnp.sum(top_p, axis=-1, keepdims=True)
        gates = jnp.zeros((T, e), xf.dtype).at[jnp.arange(T)[:, None], top_i].add(top_p)
        h = jax.nn.silu(jnp.einsum('td,edf->etf', xf, w1)) * jnp.einsum('td,edf->etf', xf, w3)
        expert_out = jnp.einsum('etf,efd->etd', h, w2)
        out = jnp.einsum('te,etd->td', gates, expert_out)
        return out.reshape(b, s, d)
    x = x + _L0_xattn_ref(ctx_1024, ctx_1024, _layernorm(x, axis=-1), L0_xattn_Wk, L0_xattn_Wv, L0_xattn_bv, L0_xattn_Wq, L0_xattn_bq, L0_xattn_Wo, L0_xattn_bo)
    x = x + _L0_ffn_ref(_layernorm(x, axis=-1), L0_ffn_router_w, L0_ffn_router_b, L0_ffn_w1, L0_ffn_w3, L0_ffn_w2)
    return x

_drawn_inputs = setup_inputs


def setup_inputs(seed=0):
    import zlib

    import numpy as np

    out = dict(_drawn_inputs(seed))
    spreads = {'L0_xattn_bv': (0.0, 0.1),
     'L0_xattn_bq': (0.0, 0.31),
     'L0_xattn_bo': (0.0, 0.1),
     'L0_ffn_router_b': (0.0, 0.8)}
    factors = {'L0_ffn_router_w': 8.0, 'L0_ffn_w1': 7.356, 'L0_ffn_w3': 7.36, 'L0_ffn_w2': 7.332}
    for name, (base, spread) in spreads.items():
        noise = np.random.default_rng([zlib.crc32(name.encode()), seed]).standard_normal(out[name].shape)
        drawn = base * np.exp(spread * noise) if base else spread * noise
        out[name] = jnp.asarray(drawn.astype(out[name].dtype))
    for name, factor in factors.items():
        out[name] = (out[name] * factor).astype(out[name].dtype)
    return out
```

```python
import concourse.bass as bass
from concourse import mybir
from contextlib import ExitStack

F32 = mybir.dt.float32
F32R = mybir.dt.float32r
ALU = mybir.AluOpType
ACT = mybir.ActivationFunctionType
AXX = mybir.AxisListType.X


def xattn_moe_program(nc, x, ctx, wk, wv, bv, wq, bq, wo, bo, rw, rb, w1, w3, w2, out):
    B, S, D = x.shape
    KC = ctx.shape[1]
    E, _, F = w1.shape
    P = 128
    NJ = S // P
    NT = B * NJ
    FULL = KC // P
    TAIL = KC - FULL * P
    NCH = FULL + 1
    KPAD = KC + KC % 2
    NG = -(-NCH // 4)
    HALVES = 2
    HT = NT // HALVES * P
    TPH = HT // P
    BPH = B // HALVES
    FC = F // P
    UNITS = HALVES * E * FC
    SPLIT_A = 1024
    PV_CUT = 7
    EPS = 1e-5
    SCALE = 1.0 / float(D) ** 0.5

    def group_chunks(g):
        return range(4 * g, min(4 * g + 4, NCH))

    def chunk_rows(c):
        return P if c < FULL else TAIL

    stack = ExitStack()
    with stack:
        def sb(name, shape, dt=F32):
            return stack.enter_context(nc.sbuf_tensor(name, shape, dt))

        def ps(name, cols):
            return stack.enter_context(nc.psum_tensor(name, [P, cols], F32))

        def sem(name):
            return stack.enter_context(nc.semaphore(name))

        x_sb = sb("x_sb", [P, NT, D])
        x_bias = sb("x_bias", [P, NT, D])
        x2 = sb("x2", [P, NT, D])
        xn1 = sb("xn1", [P, NJ, D])
        xn2 = sb("xn2", [P, NJ, D])
        ctx_sb = sb("ctx_sb", [P, B, NCH, D])
        ctxT_hi = sb("ctxT_hi", [P, 2, KPAD], F32R)
        ctxT_lo = sb("ctxT_lo", [P, 2, KPAD], F32R)
        probs = sb("probs", [P, 2, KPAD])
        probsT = sb("probsT", [P, 2, NCH, S])
        xn1T = sb("xn1T", [P, S])
        q_f = sb("q_f", [P, S])
        q_hi = sb("q_hi", [P, 2, S], F32R)
        q_lo = sb("q_lo", [P, 2, S], F32R)
        pcT = sb("pcT", [P, S])
        xn2T_hi = sb("xn2T_hi", [P, NT * P], F32R)
        xn2T_lo = sb("xn2T_lo", [P, NT * P], F32R)
        ident = sb("ident", [P, P])
        ones_row = sb("ones_row", [1, P])
        wq_sb = sb("wq_sb", [P, D])
        wk_sb = sb("wk_sb", [P, D])
        wv_sb = sb("wv_sb", [P, D])
        wo_sb = sb("wo_sb", [P, D])
        woT = sb("woT", [P, D])
        qk_w = sb("qk_w", [P, D])
        vo_w = sb("vo_w", [P, D])
        q_bias = sb("q_bias", [P, 1])
        out_bias = sb("out_bias", [P, D])
        bq_sb = sb("bq_sb", [P, 1])
        bv_sb = sb("bv_sb", [P, 1])
        bo_sb = sb("bo_sb", [1, D])
        rw_sb = sb("rw_sb", [P, E])
        rw_hi = sb("rw_hi", [P, E], F32R)
        rw_lo = sb("rw_lo", [P, E], F32R)
        rb_sb = sb("rb_sb", [P, E])
        row_max = sb("row_max", [P, NT, 2])
        neg_max = sb("neg_max", [P, NT])
        exp_sum = sb("exp_sum", [P, NT, 2])
        denom = sb("denom", [P, NT])
        rdenom = sb("rdenom", [P, NT])
        stats = sb("stats", [P, 2, NJ, 6])
        mean_var = sb("mean_var", [P, 2, NJ, 2])
        var_eps = sb("var_eps", [P, 2, NJ])
        rstd = sb("rstd", [P, 2, NJ])
        neg_half = sb("neg_half", [P, NJ])
        euler = sb("euler", [P, TPH * E])
        below = sb("below", [P, E, E])
        logits = sb("logits", [P, NT, E])
        top = sb("top", [P, TPH])
        shifted = sb("shifted", [P, TPH, E])
        ex = sb("ex", [P, TPH, E])
        greater = sb("greater", [P, TPH, E, E])
        equal = sb("equal", [P, TPH, E, E])
        beaten = sb("beaten", [P, TPH, E, E])
        rank = sb("rank", [P, TPH, E])
        kept = sb("kept", [P, TPH, E])
        kept_sum = sb("kept_sum", [P, TPH])
        rkept = sb("rkept", [P, TPH])
        gates = sb("gates", [P, TPH, E])
        gate_rows = sb("gate_rows", [P, E, HT])
        RAW = 4
        w_raw = sb("w_raw", [P, RAW, F])
        w_hi = sb("w_hi", [P, E, 3, F], F32R)
        w_lo = sb("w_lo", [P, E, 3, F], F32R)
        act_a = probs[:, 0, 0:2 * HT].rearrange("p (n t) -> p n t", t=HT)
        gated = probs[:, 1, 0:2 * HT].rearrange("p (n t) -> p n t", t=HT)
        h_f = probsT[:, 0, :, :].rearrange("p c q -> p (c q)")[:, 0:3 * HT].rearrange("p (n t) -> p n t", t=HT)
        h_hi = sb("h_hi", [P, 3, HT], F32R)
        h_lo = sb("h_lo", [P, 3, HT], F32R)
        moeT = sb("moeT", [P, HT])
        y_sb = x_sb

        scores = ps("scores", 2048)
        transit = [ps("transit0", 512), ps("transit1", 512)]
        acc = [ps("acc0", 512), ps("acc1", 512)]
        a_ps = [scores[:, 0:HT], scores[:, 512:512 + HT]]
        b_ps = [scores[:, 1024:1024 + HT], scores[:, 1536:1536 + HT]]

        x0_loaded, x_loaded = sem("x0_loaded"), sem("x_loaded")
        wqk_loaded, wvo_loaded, small_loaded = sem("wqk_loaded"), sem("wvo_loaded"), sem("small_loaded")
        ctx_loaded = [sem(f"ctx_loaded{b}") for b in range(B)]
        raw_loaded = [sem(f"raw_loaded{r}") for r in range(RAW)]
        stored = sem("stored")
        consts_ready = sem("consts_ready")
        pool_step = sem("pool_step")
        setup_mm = sem("setup_mm")
        setup_read = sem("setup_read")
        filled = sem("filled")
        act_took = sem("act_took")
        dve_took = sem("dve_took")
        scored = sem("scored")
        max_ready = sem("max_ready")
        exped = sem("exped")
        pv_done = sem("pv_done")
        pc_copied = sem("pc_copied")
        q_split = sem("q_split")
        var1_ready, rstd1_ready, xn1_ready = sem("var1_ready"), sem("rstd1_ready"), sem("xn1_ready")
        var2_ready, rstd2_ready, xn2_ready = sem("var2_ready"), sem("rstd2_ready"), sem("xn2_ready")
        bias_ready, xbias_ready = sem("bias_ready"), sem("xbias_ready")
        shift_ready, ex_ready, gates_ready = sem("shift_ready"), sem("ex_ready"), sem("gates_ready")
        wh_ready, wl_ready = sem("wh_ready"), sem("wl_ready")
        a_done, b_done, y_done = sem("a_done"), sem("b_done"), sem("y_done")
        silu_done, h_done, hh_done, hl_done = sem("silu_done"), sem("h_done"), sem("hh_done"), sem("hl_done")
        y_taken, moe_ready = sem("y_taken"), sem("moe_ready")
        dve_step = sem("dve_step")

        READERS = {"xn1T": "A", "q": "A", "ctxT": "AD", "probsT": "A", "attn": "D", "xn2T": "AD",
                   "logits": "D", "gate": "A", "outT": "D"}
        slots = [("xn1T", 0), ("q", 0)] + [("ctxT", 0, g) for g in range(NG)]
        for b in range(B + 1):
            last, first = 2 * b - 1, 2 * b
            if b >= 1:
                slots += [("probsT", last, 0), ("probsT", last, 1), ("probsT", last, 2), ("probsT", last, 3)]
            if b >= 2:
                slots += [("attn", b - 2)]
            if b >= 3:
                slots += [("logits", b - 3)]
            if b < B:
                slots += [("probsT", first, g) for g in range(NG)]
            if b + 1 < B:
                slots += [("ctxT", b + 1, 0), ("ctxT", b + 1, 1), ("xn1T", b + 1),
                          ("ctxT", b + 1, 2), ("ctxT", b + 1, 3), ("q", b + 1)]
            if b >= 2:
                slots += [("xn2T", b - 2)]
        late = {1: [("logits", 2), ("attn", 3)], 3: [("gate", 0, 0)], 4: [("gate", 0, 1), ("xn2T", 3)],
                5: [("gate", 0, 2)], 6: [("gate", 0, 3)], 7: [("logits", 3)],
                13: [("gate", 1, 0)], 14: [("gate", 1, 1)], 17: [("gate", 1, 2)], 20: [("outT", 0)],
                21: [("gate", 1, 3)], UNITS: [("outT", 1)]}
        for u in sorted(late):
            slots += late[u]
        place = {s: n for n, s in enumerate(slots)}

        def bank(s):
            return transit[place[s] % 2]

        def takes(s, reader):
            return sum(reader in READERS[k[0]] for k in slots[:place[s] + 1])

        def unit(n):
            half, e, c = n // (E * FC), n // FC % E, n % FC
            return half, e, c

        block = stack.enter_context(nc.Block())

        @block.sync
        def _(sp):
            xv = x.rearrange("b (p j) d -> p b j d", j=NJ)
            ov = out.rearrange("b (p j) d -> p b j d", j=NJ)
            xs = x_sb[:, :, :].rearrange("p (b j) d -> p b j d", j=NJ)
            ys = y_sb[:, :, :].rearrange("p (b j) d -> p b j d", j=NJ)

            def load_ctx(b):
                sp.dma_start(ctx_sb[:, b, 0:FULL, :],
                             ctx[b, 0:FULL * P, :].rearrange("(p c) d -> p c d", c=FULL)).then_inc(ctx_loaded[b], 16)
                sp.dma_start(ctx_sb[0:TAIL, b, FULL, :], ctx[b, FULL * P:KC, :]).then_inc(ctx_loaded[b], 16)

            sp.dma_start(xs[:, 0], xv[:, 0]).then_inc(x0_loaded, 16)
            sp.dma_start(wq_sb[:, :], wq).then_inc(wqk_loaded, 16)
            sp.dma_start(wk_sb[:, :], wk).then_inc(wqk_loaded, 16)
            sp.dma_start(bq_sb[:, :], bq.rearrange("(p o) -> p o", o=1)).then_inc(wqk_loaded, 16)
            load_ctx(0)
            sp.dma_start(xs[:, 1:B], xv[:, 1:B]).then_inc(x_loaded, 16)
            sp.dma_start(wv_sb[:, :], wv).then_inc(wvo_loaded, 16)
            sp.dma_start(wo_sb[:, :], wo).then_inc(wvo_loaded, 16)
            sp.dma_start(bv_sb[:, :], bv.rearrange("(p o) -> p o", o=1)).then_inc(wvo_loaded, 16)
            sp.dma_start(bo_sb[:, :], bo.rearrange("(o d) -> o d", o=1)).then_inc(wvo_loaded, 16)
            load_ctx(1)
            sp.dma_start(rw_sb[:, :], rw).then_inc(small_loaded, 16)
            sp.dma_start(rb_sb[:, :], rb.rearrange("(o e) -> o e", o=1).broadcast_to([P, E])).then_inc(small_loaded, 16)
            load_ctx(2)
            load_ctx(3)
            for k in range(3 * E):
                e, which = k // 3, k % 3
                if k >= RAW:
                    sp.wait_ge(wl_ready, k - RAW + 1)
                src = (w1[e], w3[e], w2[e].rearrange("(c p) d -> p c d", p=P))[which]
                dst = w_raw[:, k % RAW, :]
                if which == 2:
                    dst = dst.rearrange("p (c d) -> p c d", d=D)
                sp.dma_start(dst, src).then_inc(raw_loaded[k % RAW], 16)
            for half in range(HALVES):
                sp.wait_ge(dve_took, takes(("outT", half), "D"))
                hs = slice(half * BPH, (half + 1) * BPH)
                sp.dma_start(ov[:, hs], ys[:, hs]).then_inc(stored, 16)
            sp.wait_ge(stored, 16 * HALVES)

        @block.gpsimd
        def _(pool):
            def rstd_of(ln, var_sem, rstd_sem, count):
                pool.wait_ge(var_sem, count)
                nc.gpsimd.tensor_tensor(rstd[:, ln, :], var_eps[:, ln, :], neg_half[:, :], ALU.pow).then_inc(rstd_sem, 1)

            def weight_low(k):
                pool.wait_ge(wh_ready, k + 1)
                e, which = k // 3, k % 3
                nc.gpsimd.tensor_tensor(w_lo[:, e, which, :], w_raw[:, k % RAW, :],
                                        w_hi[:, e, which, :].bitcast(F32), ALU.subtract).then_inc(wl_ready, 1)

            def gate_exp(half):
                pool.wait_ge(shift_ready, half + 1)
                nc.gpsimd.tensor_tensor(ex[:, :, :].rearrange("p t e -> p (t e)"), euler[:, :],
                                        shifted[:, :, :].rearrange("p t e -> p (t e)"), ALU.pow).then_inc(ex_ready, 1)

            nc.gpsimd.memset(ident[:, :], 0.0).then_inc(pool_step, 1)
            nc.gpsimd.memset(neg_half[:, :], -0.5).then_inc(pool_step, 1)
            nc.gpsimd.memset(below[:, :, :], 0.0).then_inc(pool_step, 1)
            pool.wait_ge(pool_step, 3)
            nc.gpsimd.affine_select(out=ident[:, :], in_=ident[:, :], compare_op=ALU.not_equal, fill=1.0, base=0,
                                    pattern=[[-1, P]], channel_multiplier=1).then_inc(consts_ready, 1)
            rstd_of(0, var1_ready, rstd1_ready, 1)
            nc.gpsimd.memset(ones_row[:, :], 1.0).then_inc(consts_ready, 1)
            nc.gpsimd.affine_select(out=below[:, :, :], in_=below[:, :, :], compare_op=ALU.is_ge, fill=1.0, base=0,
                                    pattern=[[-1, E], [1, E]], channel_multiplier=0).then_inc(consts_ready, 1)
            nc.gpsimd.memset(euler[:, :], 2.718281828459045).then_inc(pool_step, 1)
            pool.wait_ge(bias_ready, 1)
            pool.wait_ge(x0_loaded, 16)
            pool.wait_ge(x_loaded, 16)
            nc.gpsimd.tensor_tensor(x_bias[:, :, :], x_sb[:, :, :],
                                    out_bias[:, :].rearrange("p (o d) -> p o d", o=1).broadcast_to([P, NT, D]),
                                    ALU.add).then_inc(xbias_ready, 1)
            pool.wait_ge(pool_step, 4)
            for b in range(B + 1):
                if b + 1 < B:
                    rstd_of(0, var1_ready, rstd1_ready, b + 2)
                if b >= 2:
                    rstd_of(1, var2_ready, rstd2_ready, b - 1)
                if b < B:
                    for k in range(3 * b, 3 * b + 3):
                        weight_low(k)
            for n in range(UNITS):
                if n == 2:
                    gate_exp(0)
                if n == 3:
                    rstd_of(1, var2_ready, rstd2_ready, B)
                if n == 10:
                    gate_exp(1)
                pool.wait_ge(hh_done, n + 1)
                if n >= 3:
                    pool.wait_ge(y_done, n - 2)
                nc.gpsimd.tensor_tensor(h_lo[:, n % 3, :], h_f[:, n % 3, :], h_hi[:, n % 3, :].bitcast(F32),
                                        ALU.subtract).then_inc(hl_done, 1)

        @block.scalar
        def _(act):
            def take(s):
                act.wait_ge(filled, place[s] + 1)

            def copy(dst, src, s):
                nc.scalar.activation(dst, src, ACT.Copy).then_inc(act_took, 1)

            def take_xn1T(b):
                s = ("xn1T", b)
                take(s)
                copy(xn1T[:, :], bank(s)[:, 0:S], s)

            def take_q(b):
                s = ("q", b)
                take(s)
                if b >= 1:
                    act.wait_ge(q_split, b)
                nc.scalar.activation(q_f[:, :], bank(s)[:, 0:S], ACT.Identity, bias=q_bias[:, 0:1], scale=SCALE)
                nc.scalar.activation(q_hi[:, b % 2, :], bank(s)[:, 0:S], ACT.Identity, bias=q_bias[:, 0:1],
                                     scale=SCALE).then_inc(act_took, 1)

            def take_ctxT(b, g):
                s = ("ctxT", b, g)
                take(s)
                lo, hi = 4 * g * P, min(4 * (g + 1) * P, KC)
                copy(ctxT_hi[:, b % 2, lo:hi], bank(s)[:, 0:hi - lo], s)

            def take_probsT(t, g):
                s = ("probsT", t, g)
                take(s)
                b, j = t // NJ, t % NJ
                n, rows = len(group_chunks(g)), chunk_rows(4 * g)
                copy(probsT[0:rows, b % 2, 4 * g:4 * g + n, j * P:(j + 1) * P],
                     bank(s)[0:rows, 0:n * P].rearrange("p (c q) -> p c q", q=P), s)

            def exps(t):
                act.wait_ge(max_ready, t + 1)
                if t >= 2:
                    act.wait_ge(filled, place[("probsT", t - 2, NG - 1)] + 1)
                for h, (lo, hi) in enumerate(((0, SPLIT_A), (SPLIT_A, KC))):
                    nc.scalar.activation(probs[:, t % 2, lo:hi], scores[:, lo:hi], ACT.Exp, bias=neg_max[:, t:t + 1],
                                         accum_out=exp_sum[:, t, h:h + 1]).then_inc(exped, 1)

            def take_pc(b):
                act.wait_ge(pv_done, b + 1)
                if b >= 1:
                    act.wait_ge(filled, place[("attn", b - 1)] + 1)
                nc.scalar.activation(pcT[:, :], acc[b % 2][:, 0:S], ACT.Copy).then_inc(pc_copied, 1)

            def take_xn2T(b):
                s = ("xn2T", b)
                take(s)
                copy(xn2T_hi[:, b * S:(b + 1) * S], bank(s)[:, 0:S], s)

            def take_gate(half, e):
                s = ("gate", half, e)
                take(s)
                if half:
                    act.wait_ge(y_taken, e + 1)
                copy(gate_rows[:, e, :], bank(s)[:, 0:HT], s)

            nc.scalar.preload_act_table(ACT.Exp)
            act.wait_ge(setup_mm, 1)
            nc.scalar.activation(qk_w[:, :], scores[:, 0:D], ACT.Copy).then_inc(setup_read, 1)
            nc.scalar.activation(q_bias[:, :], scores[:, D:D + 1], ACT.Copy, scale=SCALE).then_inc(setup_read, 1)
            act.wait_ge(setup_read, 2)
            take_xn1T(0)
            take_q(0)
            for g in range(NG):
                take_ctxT(0, g)
            act.wait_ge(setup_mm, 2)
            nc.scalar.activation(woT[:, :], scores[:, 512:512 + D], ACT.Copy).then_inc(setup_read, 1)
            act.wait_ge(setup_mm, 3)
            nc.scalar.activation(vo_w[:, :], scores[:, 1024:1024 + D], ACT.Copy).then_inc(setup_read, 1)
            act.wait_ge(setup_mm, 4)
            nc.scalar.activation(out_bias[:, :], scores[:, 1536:1536 + D], ACT.Copy).then_inc(bias_ready, 1)

            for b in range(B + 1):
                if b >= 1:
                    for g in range(NG):
                        take_probsT(2 * b - 1, g)
                if b == B:
                    break
                exps(2 * b)
                for g in range(NG):
                    take_probsT(2 * b, g)
                if b + 1 < B:
                    take_ctxT(b + 1, 0)
                    take_ctxT(b + 1, 1)
                    take_xn1T(b + 1)
                exps(2 * b + 1)
                if b + 1 < B:
                    take_ctxT(b + 1, 2)
                    take_ctxT(b + 1, 3)
                    take_q(b + 1)
                if b >= 1:
                    take_pc(b - 1)
                if b >= 2:
                    take_xn2T(b - 2)

            def high(n):
                act.wait_ge(h_done, n + 1)
                if n >= 3:
                    act.wait_ge(y_done, n - 2)
                nc.scalar.activation(h_hi[:, n % 3, :], h_f[:, n % 3, :], ACT.Copy).then_inc(hh_done, 1)

            for n in range(UNITS):
                act.wait_ge(a_done, n + 1)
                if n >= 2:
                    act.wait_ge(h_done, n - 1)
                nc.scalar.activation(act_a[:, n % 2, :], a_ps[n % 2], ACT.Silu).then_inc(silu_done, 1)
                if n == 0:
                    take_pc(B - 1)
                    take_xn2T(B - 2)
                if n >= 1:
                    high(n - 1)
                for s in late.get(n, ()):
                    if s[0] == "gate":
                        take_gate(s[1], s[2])
                    if s[0] == "xn2T":
                        take_xn2T(s[1])
            high(UNITS - 1)

        @block.vector
        def _(dve):
            steps = [0]

            def then(ins):
                steps[0] += 1
                ins.then_inc(dve_step, 1)
                dve.wait_ge(dve_step, steps[0])

            def norm_stats(ln, tiles, sem_out):
                for j in range(NJ):
                    nc.vector.bn_stats(stats[:, ln, j, :], tiles[:, j, :]).then_inc(dve_step, 1)
                steps[0] += NJ
                dve.wait_ge(dve_step, steps[0])
                for j in range(NJ):
                    nc.vector.bn_aggr(mean_var[:, ln, j, :], stats[:, ln, j, :]).then_inc(dve_step, 1)
                steps[0] += NJ
                dve.wait_ge(dve_step, steps[0])
                nc.vector.tensor_scalar(var_eps[:, ln, :], mean_var[:, ln, :, 1], EPS, None, ALU.add).then_inc(sem_out, 1)

            def normalise(ln, dst, tiles, sem_in, count, sem_out):
                dve.wait_ge(sem_in, count)
                for j in range(NJ):
                    nc.vector.tensor_scalar(dst[:, j, :], tiles[:, j, :], mean_var[:, ln, j, 0:1],
                                            rstd[:, ln, j:j + 1], ALU.subtract, ALU.mult).then_inc(sem_out, 1)

            def ln1_stats(b):
                dve.wait_ge(x0_loaded if b == 0 else x_loaded, 16)
                norm_stats(0, x_sb[:, NJ * b:NJ * (b + 1), :], var1_ready)

            def ln1(b):
                if b >= 1:
                    dve.wait_ge(filled, place[("xn1T", b - 1)] + 1)
                normalise(0, xn1, x_sb[:, NJ * b:NJ * (b + 1), :], rstd1_ready, b + 1, xn1_ready)

            def maxima(t):
                for h, (lo, hi) in enumerate(((0, SPLIT_A), (SPLIT_A, KC))):
                    dve.wait_ge(scored, 2 * t + h + 1)
                    nc.vector.tensor_reduce(row_max[:, t, h:h + 1], scores[:, lo:hi], AXX, ALU.max).then_inc(dve_step, 1)
                steps[0] += 2
                dve.wait_ge(dve_step, steps[0])
                nc.vector.tensor_reduce(neg_max[:, t:t + 1], row_max[:, t, :], AXX, ALU.max,
                                        negate=True).then_inc(max_ready, 1)

            def denominators(b):
                dve.wait_ge(exped, 4 * (b + 1))
                t = slice(NJ * b, NJ * (b + 1))
                then(nc.vector.tensor_tensor(denom[:, t], exp_sum[:, t, 0], exp_sum[:, t, 1], ALU.add))
                then(nc.vector.reciprocal(rdenom[:, t], denom[:, t]))

            def ctxT_low(b, g):
                s = ("ctxT", b, g)
                dve.wait_ge(act_took, takes(s, "A"))
                lo, hi = 4 * g * P, min(4 * (g + 1) * P, KC)
                nc.vector.tensor_tensor(ctxT_lo[:, b % 2, lo:hi], bank(s)[:, 0:hi - lo],
                                        ctxT_hi[:, b % 2, lo:hi].bitcast(F32), ALU.subtract).then_inc(dve_took, 1)

            def q_low(b):
                dve.wait_ge(act_took, takes(("q", b), "A"))
                nc.vector.tensor_tensor(q_lo[:, b % 2, :], q_f[:, :], q_hi[:, b % 2, :].bitcast(F32),
                                        ALU.subtract).then_inc(q_split, 1)

            def weight_high(k):
                e, which = k // 3, k % 3
                dve.wait_ge(raw_loaded[k % RAW], 16 * (k // RAW + 1))
                nc.vector.tensor_copy(w_hi[:, e, which, :], w_raw[:, k % RAW, :]).then_inc(wh_ready, 1)

            def residual(b):
                s = ("attn", b)
                if b == 0:
                    dve.wait_ge(xbias_ready, 1)
                denominators(b)
                dve.wait_ge(filled, place[s] + 1)
                for j in range(NJ):
                    t = NJ * b + j
                    ins = nc.vector.scalar_tensor_tensor(x2[:, t, :], bank(s)[:, j * P:(j + 1) * P], rdenom[:, t:t + 1],
                                                         x_bias[:, t, :], ALU.mult, ALU.add)
                    if j == NJ - 1:
                        ins.then_inc(dve_took, 1)
                dve.wait_ge(dve_took, takes(s, "D"))
                norm_stats(1, x2[:, NJ * b:NJ * (b + 1), :], var2_ready)

            def ln2(b):
                if b >= 1:
                    dve.wait_ge(filled, place[("xn2T", b - 1)] + 1)
                normalise(1, xn2, x2[:, NJ * b:NJ * (b + 1), :], rstd2_ready, b + 1, xn2_ready)

            def xn2T_low(b):
                s = ("xn2T", b)
                dve.wait_ge(act_took, takes(s, "A"))
                c = slice(b * S, (b + 1) * S)
                nc.vector.tensor_tensor(xn2T_lo[:, c], bank(s)[:, 0:S], xn2T_hi[:, c].bitcast(F32),
                                        ALU.subtract).then_inc(dve_took, 1)

            def take_logits(b):
                s = ("logits", b)
                dve.wait_ge(filled, place[s] + 1)
                nc.vector.tensor_tensor(logits[:, NJ * b:NJ * (b + 1), :],
                                        bank(s)[:, 0:NJ * E].rearrange("p (j e) -> p j e", e=E),
                                        rb_sb[:, :].rearrange("p (o e) -> p o e", o=1).broadcast_to([P, NJ, E]),
                                        ALU.add).then_inc(dve_took, 1)
                dve.wait_ge(dve_took, takes(s, "D"))

            def rank_experts(half):
                lg = logits[:, half * TPH:(half + 1) * TPH, :]
                as_j = lg.rearrange("p t (o j) -> p t o j", o=1).broadcast_to([P, TPH, E, E])
                as_e = lg.rearrange("p t (e o) -> p t e o", o=1).broadcast_to([P, TPH, E, E])
                then(nc.vector.tensor_reduce(top[:, :], lg, AXX, ALU.max))
                nc.vector.tensor_tensor(shifted[:, :, :], lg,
                                        top[:, :].rearrange("p (t o) -> p t o", o=1).broadcast_to([P, TPH, E]),
                                        ALU.subtract).then_inc(shift_ready, 1)
                nc.vector.tensor_tensor(greater[:, :, :, :], as_j, as_e, ALU.is_gt)
                then(nc.vector.tensor_tensor(equal[:, :, :, :], as_j, as_e, ALU.is_equal))
                then(nc.vector.tensor_tensor(equal[:, :, :, :], equal[:, :, :, :],
                                             below[:, :, :].rearrange("p (o e) j -> p o e j", o=1)
                                             .broadcast_to([P, TPH, E, E]), ALU.mult))
                then(nc.vector.tensor_tensor(beaten[:, :, :, :], greater[:, :, :, :], equal[:, :, :, :], ALU.add))
                then(nc.vector.tensor_reduce(rank[:, :, :], beaten[:, :, :, :], AXX, ALU.add))

            def make_gates(half):
                dve.wait_ge(ex_ready, half + 1)
                then(nc.vector.scalar_tensor_tensor(kept[:, :, :], rank[:, :, :], 1.5, ex[:, :, :], ALU.is_lt, ALU.mult))
                then(nc.vector.tensor_reduce(kept_sum[:, :], kept[:, :, :], AXX, ALU.add))
                then(nc.vector.reciprocal(rkept[:, :], kept_sum[:, :]))
                nc.vector.tensor_tensor(gates[:, :, :], kept[:, :, :],
                                        rkept[:, :].rearrange("p (t o) -> p t o", o=1).broadcast_to([P, TPH, E]),
                                        ALU.mult).then_inc(gates_ready, 1)

            if KPAD > KC:
                nc.vector.memset(ctxT_hi[:, :, KC:KPAD].bitcast(F32), 0.0).then_inc(consts_ready, 1)
                nc.vector.memset(ctxT_lo[:, :, KC:KPAD].bitcast(F32), 0.0).then_inc(consts_ready, 1)
            ln1_stats(0)
            ln1(0)
            q_low(0)
            for g in range(NG):
                ctxT_low(0, g)
            dve.wait_ge(small_loaded, 32)
            then(nc.vector.tensor_copy(rw_hi[:, :], rw_sb[:, :]))
            then(nc.vector.tensor_tensor(rw_lo[:, :], rw_sb[:, :], rw_hi[:, :].bitcast(F32), ALU.subtract))
            dve.wait_ge(consts_ready, 5)

            for b in range(B + 1):
                if b < B:
                    maxima(2 * b)
                if b + 1 < B:
                    ln1_stats(b + 1)
                if b >= 2:
                    residual(b - 2)
                if b >= 3:
                    take_logits(b - 3)
                if b + 1 < B:
                    ln1(b + 1)
                if b >= 2:
                    ln2(b - 2)
                if b < B:
                    maxima(2 * b + 1)
                if b + 1 < B:
                    ctxT_low(b + 1, 0)
                    ctxT_low(b + 1, 1)
                if b < B:
                    for k in range(3 * b, 3 * b + 3):
                        weight_high(k)
                if b + 1 < B:
                    ctxT_low(b + 1, 2)
                    ctxT_low(b + 1, 3)
                    q_low(b + 1)
                if 2 <= b < B:
                    xn2T_low(b - 2)

            def combine(k):
                half, e = k // E, k % E
                dve.wait_ge(y_done, FC * (k + 1))
                dve.wait_ge(act_took, takes(("gate", half, e), "A"))
                ins = nc.vector.tensor_tensor(moeT[:, :] if e == 0 else gated[:, k % 2, :],
                                              acc[k % 2][:, 0:HT], gate_rows[:, e, :], ALU.mult)
                ins.then_inc(y_taken, 1)
                if e:
                    dve.wait_ge(y_taken, k + 1)
                    ins = nc.vector.tensor_tensor(moeT[:, :], moeT[:, :], gated[:, k % 2, :], ALU.add)
                    if e == E - 1:
                        ins.then_inc(moe_ready, 1)
                    else:
                        then(ins)

            def finish(half):
                s = ("outT", half)
                dve.wait_ge(filled, place[s] + 1)
                t = slice(half * TPH, (half + 1) * TPH)
                nc.vector.tensor_tensor(y_sb[:, t, :], bank(s)[:, 0:HT].rearrange("p (t d) -> p t d", d=D),
                                        x2[:, t, :], ALU.add).then_inc(dve_took, 1)

            for n in range(UNITS):
                dve.wait_ge(silu_done, n + 1)
                dve.wait_ge(b_done, n + 1)
                if n >= 3:
                    dve.wait_ge(hl_done, n - 2)
                nc.vector.tensor_tensor(h_f[:, n % 3, :], b_ps[n % 2], act_a[:, n % 2, :], ALU.mult).then_inc(h_done, 1)
                if n == 0:
                    xn2T_low(B - 2)
                    rank_experts(0)
                if n == 1:
                    take_logits(2)
                    residual(3)
                if n == 2:
                    make_gates(0)
                if n == 3:
                    ln2(3)
                if n == 5:
                    xn2T_low(3)
                if n == 8:
                    take_logits(3)
                    rank_experts(1)
                if n == 10:
                    make_gates(1)
                if n >= 6 and n % FC == 2:
                    combine((n - 6) // FC)
                if n == 21:
                    finish(0)
            combine(2 * E - 1)
            finish(1)

        @block.tensor
        def _(pe):
            def open_slot(s):
                n = place[s]
                if n >= 2:
                    old = slots[n - 2]
                    if READERS[old[0]].endswith("D"):
                        pe.wait_ge(dve_took, takes(old, "D"))
                    else:
                        pe.wait_ge(act_took, takes(old, "A"))

            def matmul3(dst, lhs_hi, lhs_lo, rhs_hi, rhs_lo, first=True, last=True):
                nc.tensor.matmul(dst, lhs_hi, rhs_hi, start=first, stop=False)
                nc.tensor.matmul(dst, lhs_hi, rhs_lo, start=False, stop=False)
                return nc.tensor.matmul(dst, lhs_lo, rhs_hi, start=False, stop=last)

            def fill_xn1T(b):
                s = ("xn1T", b)
                open_slot(s)
                pe.wait_ge(xn1_ready, NJ * (b + 1))
                for j in range(NJ):
                    ins = nc.tensor.transpose(bank(s)[:, j * P:(j + 1) * P], xn1[:, j, :], ident[:, :])
                ins.then_inc(filled, 1)

            def fill_q(b):
                s = ("q", b)
                open_slot(s)
                pe.wait_ge(act_took, takes(("xn1T", b), "A"))
                nc.tensor.matmul(bank(s)[:, 0:S], qk_w[:, :], xn1T[:, :], start=True, stop=True).then_inc(filled, 1)

            def fill_ctxT(b, g):
                s = ("ctxT", b, g)
                open_slot(s)
                if g == 0:
                    pe.wait_ge(ctx_loaded[b], 32)
                for i, c in enumerate(group_chunks(g)):
                    r = chunk_rows(c)
                    ins = nc.tensor.transpose(bank(s)[:, i * P:i * P + r], ctx_sb[0:r, b, c, :], ident[0:r, 0:r])
                ins.then_inc(filled, 1)

            def fill_probsT(t, g):
                s = ("probsT", t, g)
                open_slot(s)
                pe.wait_ge(exped, 2 * t + (1 if 4 * (g + 1) * P <= SPLIT_A else 2))
                for i, c in enumerate(group_chunks(g)):
                    r = chunk_rows(c)
                    ins = nc.tensor.transpose(bank(s)[0:r, i * P:(i + 1) * P],
                                              probs[:, t % 2, c * P:c * P + r], ident[:, :])
                ins.then_inc(filled, 1)

            def score(t, h):
                b, j = t // NJ, t % NJ
                if j == 0 and h == 0:
                    pe.wait_ge(q_split, b + 1)
                    pe.wait_ge(dve_took, takes(("ctxT", b, NG - 1), "D"))
                if t >= 1:
                    pe.wait_ge(exped, 2 * t - 1 + h)
                lo, end = (0, SPLIT_A) if h == 0 else (SPLIT_A, KPAD)
                q = slice(j * P, (j + 1) * P)
                while lo < end:
                    hi = min(lo + 512, end)
                    ins = matmul3(scores[:, lo:hi], q_hi[:, b % 2, q], q_lo[:, b % 2, q],
                                  ctxT_hi[:, b % 2, lo:hi], ctxT_lo[:, b % 2, lo:hi])
                    lo = hi
                ins.then_inc(scored, 1)

            def values(b, first, end):
                if first == 0:
                    pe.wait_ge(act_took, takes(("probsT", NJ * b + 1, NG - 1), "A"))
                    if b >= 2:
                        pe.wait_ge(pc_copied, b - 1)
                for c in range(first, end):
                    r = chunk_rows(c)
                    ins = nc.tensor.matmul(acc[b % 2][:, 0:S], ctx_sb[0:r, b, c, :], probsT[0:r, b % 2, c, :],
                                           start=(c == 0), stop=(c == NCH - 1))
                if end == NCH:
                    ins.then_inc(pv_done, 1)

            def fill_attn(b):
                s = ("attn", b)
                open_slot(s)
                pe.wait_ge(pc_copied, b + 1)
                for j in range(NJ):
                    ins = nc.tensor.matmul(bank(s)[:, j * P:(j + 1) * P], pcT[:, j * P:(j + 1) * P], vo_w[:, :],
                                           start=True, stop=True)
                ins.then_inc(filled, 1)

            def fill_xn2T(b):
                s = ("xn2T", b)
                open_slot(s)
                pe.wait_ge(xn2_ready, NJ * (b + 1))
                for j in range(NJ):
                    ins = nc.tensor.transpose(bank(s)[:, j * P:(j + 1) * P], xn2[:, j, :], ident[:, :])
                ins.then_inc(filled, 1)

            def fill_logits(b):
                s = ("logits", b)
                open_slot(s)
                pe.wait_ge(dve_took, takes(("xn2T", b), "D"))
                for j in range(NJ):
                    q = slice(b * S + j * P, b * S + (j + 1) * P)
                    ins = matmul3(bank(s)[:, j * E:(j + 1) * E], xn2T_hi[:, q], xn2T_lo[:, q], rw_hi[:, :], rw_lo[:, :])
                ins.then_inc(filled, 1)

            def fill_gate(half, e):
                s = ("gate", half, e)
                open_slot(s)
                pe.wait_ge(gates_ready, half + 1)
                for t in range(TPH):
                    ins = nc.tensor.transpose(bank(s)[:, t * P:(t + 1) * P],
                                              gates[:, t, e:e + 1].broadcast_to([P, P]), ident[:, :])
                ins.then_inc(filled, 1)

            def fill_outT(half):
                s = ("outT", half)
                open_slot(s)
                pe.wait_ge(moe_ready, half + 1)
                for t in range(TPH):
                    ins = nc.tensor.transpose(bank(s)[:, t * P:(t + 1) * P], moeT[:, t * P:(t + 1) * P], ident[:, :])
                ins.then_inc(filled, 1)

            FILL = {"logits": fill_logits, "attn": fill_attn, "gate": fill_gate, "xn2T": fill_xn2T, "outT": fill_outT}

            pe.wait_ge(wqk_loaded, 48)
            nc.tensor.matmul(scores[:, 0:D], wq_sb[:, :], wk_sb[:, :], start=True, stop=True)
            nc.tensor.matmul(scores[:, D:D + 1], wk_sb[:, :], bq_sb[:, :], start=True, stop=True).then_inc(setup_mm, 1)
            pe.wait_ge(consts_ready, 1)
            fill_xn1T(0)
            pe.wait_ge(setup_read, 2)
            fill_q(0)
            for g in range(NG):
                fill_ctxT(0, g)
            pe.wait_ge(wvo_loaded, 64)
            nc.tensor.transpose(scores[:, 512:512 + D], wo_sb[:, :], ident[:, :]).then_inc(setup_mm, 1)
            pe.wait_ge(setup_read, 3)
            nc.tensor.matmul(scores[:, 1024:1024 + D], wv_sb[:, :], woT[:, :], start=True, stop=True).then_inc(setup_mm, 1)
            pe.wait_ge(consts_ready, 5)
            nc.tensor.matmul(scores[:, 1536:1536 + D], bv_sb[:, 0:1].broadcast_to([P, P]), woT[:, :], start=True, stop=False)
            nc.tensor.matmul(scores[:, 1536:1536 + D], ones_row[:, :], bo_sb[:, :], start=False, stop=True).then_inc(setup_mm, 1)
            pe.wait_ge(bias_ready, 1)

            def expert_in(n):
                half, e, c = unit(n)
                tok = slice(half * HT, (half + 1) * HT)
                f = slice(c * P, (c + 1) * P)
                if n % FC == 0 and half == 0:
                    pe.wait_ge(wl_ready, 3 * (e + 1))
                if n % (E * FC) == 0:
                    pe.wait_ge(dve_took, takes(("xn2T", BPH * (half + 1) - 1), "D"))
                if n >= 2:
                    pe.wait_ge(silu_done, n - 1)
                matmul3(a_ps[n % 2], w_hi[:, e, 0, f], w_lo[:, e, 0, f], xn2T_hi[:, tok], xn2T_lo[:, tok]).then_inc(a_done, 1)
                if n >= 2:
                    pe.wait_ge(h_done, n - 1)
                matmul3(b_ps[n % 2], w_hi[:, e, 1, f], w_lo[:, e, 1, f], xn2T_hi[:, tok], xn2T_lo[:, tok]).then_inc(b_done, 1)

            def expert_out(n):
                half, e, c = unit(n)
                k = n // FC
                if c == 0 and k >= 2:
                    pe.wait_ge(y_taken, k - 1)
                if k < 2 and c == 0:
                    pe.wait_ge(pc_copied, B - 1 + k)
                pe.wait_ge(hl_done, n + 1)
                d = slice(c * D, (c + 1) * D)
                matmul3(acc[k % 2][:, 0:HT], w_hi[:, e, 2, d], w_lo[:, e, 2, d], h_hi[:, n % 3, :], h_lo[:, n % 3, :],
                        first=(c == 0), last=(c == FC - 1)).then_inc(y_done, 1)

            for b in range(B + 1):
                if b >= 1:
                    fill_probsT(2 * b - 1, 0)
                    fill_probsT(2 * b - 1, 1)
                if b < B:
                    score(2 * b, 0)
                if b >= 1:
                    fill_probsT(2 * b - 1, 2)
                    fill_probsT(2 * b - 1, 3)
                if b < B:
                    score(2 * b, 1)
                if b >= 2:
                    fill_attn(b - 2)
                if b >= 3:
                    fill_logits(b - 3)
                if b >= 1:
                    values(b - 1, 0, PV_CUT)
                if b < B:
                    fill_probsT(2 * b, 0)
                    fill_probsT(2 * b, 1)
                    score(2 * b + 1, 0)
                    fill_probsT(2 * b, 2)
                    fill_probsT(2 * b, 3)
                    score(2 * b + 1, 1)
                if b + 1 < B:
                    fill_ctxT(b + 1, 0)
                    fill_ctxT(b + 1, 1)
                    fill_xn1T(b + 1)
                if b >= 1:
                    values(b - 1, PV_CUT, NCH)
                if b + 1 < B:
                    fill_ctxT(b + 1, 2)
                    fill_ctxT(b + 1, 3)
                    fill_q(b + 1)
                if b >= 2:
                    fill_xn2T(b - 2)

            for n in range(UNITS):
                expert_in(n)
                if n >= 2:
                    expert_out(n - 2)
                for s in late.get(n, ()):
                    FILL[s[0]](*s[1:])
            expert_out(UNITS - 2)
            expert_out(UNITS - 1)
            for s in late[UNITS]:
                FILL[s[0]](*s[1:])


_INS = ["x", "ctx_1024", "L0_xattn_Wk", "L0_xattn_Wv", "L0_xattn_bv", "L0_xattn_Wq", "L0_xattn_bq", "L0_xattn_Wo",
        "L0_xattn_bo", "L0_ffn_router_w", "L0_ffn_router_b", "L0_ffn_w1", "L0_ffn_w3", "L0_ffn_w2"]


def kernel(**inputs):
    import numpy as np
    import concourse.bacc as bacc
    from concourse import mybir as mb
    from concourse.bass_utils import run_bass_kernel_spmd as run

    nc = bacc.Bacc("TRN2", target_bir_lowering=False, num_devices=1)
    arrays, args = {}, []
    for name in _INS:
        a = np.ascontiguousarray(inputs[name])
        arrays[f"in_{name}_dram"] = a
        args.append(nc.dram_tensor(f"in_{name}_dram", a.shape, mb.dt.from_np(a.dtype), kind="ExternalInput").ap())
    shape = inputs["x"].shape
    out = nc.dram_tensor("out_dram", shape, mb.dt.float32, kind="ExternalOutput").ap()
    xattn_moe_program(nc, *args, out)
    r = run(nc, [arrays], core_ids=[0])
    return r.results[0]["out_dram"]
```

```python
import concourse.bass as bass
from concourse import mybir
from contextlib import ExitStack

F32 = mybir.dt.float32
F32R = mybir.dt.float32r
ALU = mybir.AluOpType
ACT = mybir.ActivationFunctionType
AXX = mybir.AxisListType.X


def xattn_moe_program(nc, x, ctx, wk, wv, bv, wq, bq, wo, bo, rw, rb, w1, w3, w2, out):
    B, S, D = x.shape
    KC = ctx.shape[1]
    E, _, F = w1.shape
    P = 128
    NJ = S // P
    NT = B * NJ
    FULL = KC // P
    TAIL = KC - FULL * P
    NCH = FULL + 1
    KPAD = KC + KC % 2
    NG = -(-NCH // 4)
    HALVES = 2
    HT = NT // HALVES * P
    TPH = HT // P
    BPH = B // HALVES
    FC = F // P
    UNITS = HALVES * E * FC
    BANK = 512
    SPLIT_A = 2 * BANK
    LOW_ON_DVE = (10, 11)
    EPS = 1e-5
    SCALE = 1.0 / float(D) ** 0.5

    def group_chunks(g):
        return range(4 * g, min(4 * g + 4, NCH))

    def chunk_rows(c):
        return P if c < FULL else TAIL

    stack = ExitStack()
    with stack:
        def sb(name, shape, dt=F32):
            return stack.enter_context(nc.sbuf_tensor(name, shape, dt))

        def ps(name, cols):
            return stack.enter_context(nc.psum_tensor(name, [P, cols], F32))

        def sem(name):
            return stack.enter_context(nc.semaphore(name))

        x_sb = sb("x_sb", [P, NT, D])
        x_bias = sb("x_bias", [P, NT, D])
        x2 = sb("x2", [P, NT, D])
        xn1 = sb("xn1", [P, NJ, D])
        xn2 = sb("xn2", [P, NJ, D])
        ctx_sb = sb("ctx_sb", [P, B, NCH, D])
        ctxT_hi = sb("ctxT_hi", [P, 2, KPAD], F32R)
        ctxT_lo = sb("ctxT_lo", [P, 2, KPAD], F32R)
        probs = sb("probs", [P, 2, KPAD])
        probsT = sb("probsT", [P, 2, NCH, S])
        xn1T = sb("xn1T", [P, S])
        q_f = sb("q_f", [P, S])
        q_hi = sb("q_hi", [P, 2, S], F32R)
        q_lo = sb("q_lo", [P, 2, S], F32R)
        pcT = sb("pcT", [P, S])
        xn2T_hi = sb("xn2T_hi", [P, NT * P], F32R)
        xn2T_lo = sb("xn2T_lo", [P, NT * P], F32R)
        ident = sb("ident", [P, P])
        ones_row = sb("ones_row", [1, P])
        wq_sb = sb("wq_sb", [P, D])
        wk_sb = sb("wk_sb", [P, D])
        wv_sb = sb("wv_sb", [P, D])
        wo_sb = sb("wo_sb", [P, D])
        woT = sb("woT", [P, D])
        qk_w = sb("qk_w", [P, D])
        vo_w = sb("vo_w", [P, D])
        q_bias = sb("q_bias", [P, 1])
        out_bias = sb("out_bias", [P, D])
        bq_sb = sb("bq_sb", [P, 1])
        bv_sb = sb("bv_sb", [P, 1])
        bo_sb = sb("bo_sb", [1, D])
        rw_sb = sb("rw_sb", [P, E])
        rw_hi = sb("rw_hi", [P, E], F32R)
        rw_lo = sb("rw_lo", [P, E], F32R)
        rb_sb = sb("rb_sb", [P, E])
        row_max = sb("row_max", [P, NT, 2])
        neg_max = sb("neg_max", [P, NT])
        exp_sum = sb("exp_sum", [P, NT, 2])
        denom = sb("denom", [P, NT])
        rdenom = sb("rdenom", [P, NT])
        stats = sb("stats", [P, 2, NJ, 6])
        mean_var = sb("mean_var", [P, 2, NJ, 2])
        var_eps = sb("var_eps", [P, 2, NJ])
        rstd = sb("rstd", [P, 2, NJ])
        neg_half = sb("neg_half", [P, NJ])
        euler = sb("euler", [P, TPH * E])
        below = sb("below", [P, E, E])
        logits = sb("logits", [P, NT, E])
        top = sb("top", [P, TPH])
        shifted = sb("shifted", [P, TPH, E])
        ex = sb("ex", [P, TPH, E])
        greater = sb("greater", [P, TPH, E, E])
        equal = sb("equal", [P, TPH, E, E])
        beaten = sb("beaten", [P, TPH, E, E])
        rank = sb("rank", [P, TPH, E])
        kept = sb("kept", [P, TPH, E])
        kept_sum = sb("kept_sum", [P, TPH])
        rkept = sb("rkept", [P, TPH])
        gates = sb("gates", [P, TPH, E])
        gate_rows = sb("gate_rows", [P, E, HT])
        RAW = 4
        w_raw = sb("w_raw", [P, RAW, F])
        w_hi = sb("w_hi", [P, E, 3, F], F32R)
        w_lo = sb("w_lo", [P, E, 3, F], F32R)
        act_a = probs[:, 0, 0:2 * HT].rearrange("p (n t) -> p n t", t=HT)
        gated = probs[:, 1, 0:2 * HT].rearrange("p (n t) -> p n t", t=HT)
        h_f = probsT[:, 0, :, :].rearrange("p c q -> p (c q)")[:, 0:3 * HT].rearrange("p (n t) -> p n t", t=HT)
        h_hi = sb("h_hi", [P, 3, HT], F32R)
        h_lo = sb("h_lo", [P, 3, HT], F32R)
        moeT = sb("moeT", [P, HT])
        y_sb = x_sb

        scores = ps("scores", 2048)
        transit = [ps("transit0", 512), ps("transit1", 512)]
        acc = [ps("acc0", 512), ps("acc1", 512)]
        a_ps = [scores[:, 0:HT], scores[:, 512:512 + HT]]
        b_ps = [scores[:, 1024:1024 + HT], scores[:, 1536:1536 + HT]]

        x0_loaded, x_loaded = sem("x0_loaded"), sem("x_loaded")
        wqk_loaded, wvo_loaded, small_loaded = sem("wqk_loaded"), sem("wvo_loaded"), sem("small_loaded")
        ctx_loaded = [(sem(f"ctx_first{b}"), sem(f"ctx_rest{b}")) for b in range(B)]
        raw_loaded = [sem(f"raw_loaded{r}") for r in range(RAW)]
        stored = sem("stored")
        consts_ready = sem("consts_ready")
        pool_step = sem("pool_step")
        setup_mm = sem("setup_mm")
        setup_read = sem("setup_read")
        filled = sem("filled")
        act_took = sem("act_took")
        dve_took = sem("dve_took")
        scored = sem("scored")
        max_ready = sem("max_ready")
        exped = sem("exped")
        pv_done = sem("pv_done")
        pc_copied = sem("pc_copied")
        q_split = sem("q_split")
        var1_ready, rstd1_ready, xn1_ready = sem("var1_ready"), sem("rstd1_ready"), sem("xn1_ready")
        var2_ready, rstd2_ready, xn2_ready = sem("var2_ready"), sem("rstd2_ready"), sem("xn2_ready")
        bias_ready, xbias_ready = sem("bias_ready"), sem("xbias_ready")
        shift_ready, ex_ready, gates_ready = sem("shift_ready"), sem("ex_ready"), sem("gates_ready")
        wh_ready, wl_ready = sem("wh_ready"), sem("wl_ready")
        a_done, b_done, y_done = sem("a_done"), sem("b_done"), sem("y_done")
        silu_done, h_done, hh_done, hl_done = sem("silu_done"), sem("h_done"), sem("hh_done"), sem("hl_done")
        hl_dve = sem("hl_dve")
        y_taken, moe_ready = sem("y_taken"), sem("moe_ready")
        dve_step = sem("dve_step")

        READERS = {"qk_w": "A", "woT": "A", "vo_w": "A", "out_bias": "A", "xn1T": "A", "q": "A", "ctxT": "AD", "probsT": "A", "attn": "D", "xn2T": "AD",
                   "logits": "D", "gate": "A", "outT": "D"}
        slots = [("qk_w",), ("xn1T", 0), ("q", 0)] + [("ctxT", 0, g) for g in range(NG)]
        for b in range(B + 1):
            if b >= 1:
                slots += [("probsT", 2 * b - 1, g) for g in range(NG)]
            if b == 0:
                slots += [("woT",), ("vo_w",), ("out_bias",)]
            if b + 1 < B:
                slots += [("ctxT", b + 1, 0), ("ctxT", b + 1, 1)]
            if b >= 2:
                slots += [("attn", b - 2)]
            if b >= 3:
                slots += [("logits", b - 3)]
            if b < B:
                slots += [("probsT", 2 * b, g) for g in range(NG)]
            if b + 1 < B:
                slots += [("xn1T", b + 1), ("ctxT", b + 1, 2), ("ctxT", b + 1, 3), ("q", b + 1)]
            if b >= 2:
                slots += [("xn2T", b - 2)]
        late = {2: [("logits", 2), ("attn", 3)], 3: [("gate", 0, 0)], 4: [("gate", 0, 1), ("xn2T", 3)],
                5: [("gate", 0, 2)], 6: [("gate", 0, 3)], 7: [("logits", 3)],
                13: [("gate", 1, 0)], 14: [("gate", 1, 1)], 17: [("gate", 1, 2)], 20: [("outT", 0)],
                21: [("gate", 1, 3)], UNITS: [("outT", 1)]}
        for u in sorted(late):
            slots += late[u]
        place = {s: n for n, s in enumerate(slots)}

        ring = [4 if n < place[("probsT", 1, 0)] else 2 for n in range(len(slots))]
        banks = [n % ring[n] for n in range(len(slots))]

        def bank(s):
            return (transit + acc)[banks[place[s]]]

        def before(n):
            return max((m for m in range(n) if banks[m] == banks[n]), default=None)

        def takes(s, reader):
            return sum(reader in READERS[k[0]] for k in slots[:place[s] + 1])

        def lows(n):
            return sum((m in LOW_ON_DVE) == (n in LOW_ON_DVE) for m in range(n + 1))

        def unit(n):
            half, e, c = n // (E * FC), n // FC % E, n % FC
            return half, e, c

        block = stack.enter_context(nc.Block())

        @block.sync
        def _(sp):
            xv = x.rearrange("b (p j) d -> p b j d", j=NJ)
            ov = out.rearrange("b (p j) d -> p b j d", j=NJ)
            xs = x_sb[:, :, :].rearrange("p (b j) d -> p b j d", j=NJ)
            ys = y_sb[:, :, :].rearrange("p (b j) d -> p b j d", j=NJ)

            def load_ctx(b):
                keys = ctx[b, 0:FULL * P, :].rearrange("(p c) d -> p c d", c=FULL)
                sp.dma_start(ctx_sb[:, b, 0:8, :], keys[:, 0:8, :]).then_inc(ctx_loaded[b][0], 16)
                sp.dma_start(ctx_sb[:, b, 8:FULL, :], keys[:, 8:FULL, :]).then_inc(ctx_loaded[b][1], 16)
                sp.dma_start(ctx_sb[0:TAIL, b, FULL, :], ctx[b, FULL * P:KC, :]).then_inc(ctx_loaded[b][1], 16)

            sp.dma_start(xs[:, 0], xv[:, 0]).then_inc(x0_loaded, 16)
            sp.dma_start(wq_sb[:, :], wq).then_inc(wqk_loaded, 16)
            sp.dma_start(wk_sb[:, :], wk).then_inc(wqk_loaded, 16)
            sp.dma_start(bq_sb[:, :], bq.rearrange("(p o) -> p o", o=1)).then_inc(wqk_loaded, 16)
            load_ctx(0)
            sp.dma_start(wv_sb[:, :], wv).then_inc(wvo_loaded, 16)
            sp.dma_start(wo_sb[:, :], wo).then_inc(wvo_loaded, 16)
            sp.dma_start(bv_sb[:, :], bv.rearrange("(p o) -> p o", o=1)).then_inc(wvo_loaded, 16)
            sp.dma_start(bo_sb[:, :], bo.rearrange("(o d) -> o d", o=1)).then_inc(wvo_loaded, 16)
            load_ctx(1)
            sp.dma_start(xs[:, 1:B], xv[:, 1:B]).then_inc(x_loaded, 16)
            sp.dma_start(rw_sb[:, :], rw).then_inc(small_loaded, 16)
            sp.dma_start(rb_sb[:, :], rb.rearrange("(o e) -> o e", o=1).broadcast_to([P, E])).then_inc(small_loaded, 16)
            load_ctx(2)
            load_ctx(3)
            for k in range(3 * E):
                e, which = k // 3, k % 3
                if k >= RAW:
                    sp.wait_ge(wl_ready, k - RAW + 1)
                src = (w1[e], w3[e], w2[e].rearrange("(c p) d -> p c d", p=P))[which]
                dst = w_raw[:, k % RAW, :]
                if which == 2:
                    dst = dst.rearrange("p (c d) -> p c d", d=D)
                sp.dma_start(dst, src).then_inc(raw_loaded[k % RAW], 16)
            for half in range(HALVES):
                sp.wait_ge(dve_took, takes(("outT", half), "D"))
                hs = slice(half * BPH, (half + 1) * BPH)
                sp.dma_start(ov[:, hs], ys[:, hs]).then_inc(stored, 16)
            sp.wait_ge(stored, 16 * HALVES)

        @block.gpsimd
        def _(pool):
            def rstd_of(ln, var_sem, rstd_sem, count):
                pool.wait_ge(var_sem, count)
                nc.gpsimd.tensor_tensor(rstd[:, ln, :], var_eps[:, ln, :], neg_half[:, :], ALU.pow).then_inc(rstd_sem, 1)

            def weight_low(k):
                pool.wait_ge(wh_ready, k + 1)
                e, which = k // 3, k % 3
                nc.gpsimd.tensor_tensor(w_lo[:, e, which, :], w_raw[:, k % RAW, :],
                                        w_hi[:, e, which, :].bitcast(F32), ALU.subtract).then_inc(wl_ready, 1)

            def gate_exp(half):
                pool.wait_ge(shift_ready, half + 1)
                nc.gpsimd.tensor_tensor(ex[:, :, :].rearrange("p t e -> p (t e)"), euler[:, :],
                                        shifted[:, :, :].rearrange("p t e -> p (t e)"), ALU.pow).then_inc(ex_ready, 1)

            def bias_x():
                pool.wait_ge(act_took, takes(("out_bias",), "A"))
                pool.wait_ge(x0_loaded, 16)
                pool.wait_ge(x_loaded, 16)
                nc.gpsimd.tensor_tensor(x_bias[:, :, :], x_sb[:, :, :],
                                        out_bias[:, :].rearrange("p (o d) -> p o d", o=1).broadcast_to([P, NT, D]),
                                        ALU.add).then_inc(xbias_ready, 1)

            nc.gpsimd.memset(ident[:, :], 0.0).then_inc(pool_step, 1)
            nc.gpsimd.memset(neg_half[:, :], -0.5).then_inc(pool_step, 1)
            nc.gpsimd.memset(below[:, :, :], 0.0).then_inc(pool_step, 1)
            pool.wait_ge(pool_step, 3)
            nc.gpsimd.affine_select(out=ident[:, :], in_=ident[:, :], compare_op=ALU.not_equal, fill=1.0, base=0,
                                    pattern=[[-1, P]], channel_multiplier=1).then_inc(consts_ready, 1)
            rstd_of(0, var1_ready, rstd1_ready, 1)
            nc.gpsimd.memset(ones_row[:, :], 1.0).then_inc(consts_ready, 1)
            nc.gpsimd.affine_select(out=below[:, :, :], in_=below[:, :, :], compare_op=ALU.is_ge, fill=1.0, base=0,
                                    pattern=[[-1, E], [1, E]], channel_multiplier=0).then_inc(consts_ready, 1)
            nc.gpsimd.memset(euler[:, :], 2.718281828459045).then_inc(pool_step, 1)
            for b in range(B):
                if b + 1 < B:
                    rstd_of(0, var1_ready, rstd1_ready, b + 2)
                if b == 0:
                    bias_x()
                if b >= 2:
                    rstd_of(1, var2_ready, rstd2_ready, b - 1)
                for k in range(3 * b, 3 * b + 3):
                    weight_low(k)

            def low(n):
                pool.wait_ge(hh_done, n + 1)
                if n >= 3:
                    pool.wait_ge(y_done, n - 2)
                nc.gpsimd.tensor_tensor(h_lo[:, n % 3, :], h_f[:, n % 3, :], h_hi[:, n % 3, :].bitcast(F32),
                                        ALU.subtract).then_inc(hl_done, 1)

            low(0)
            rstd_of(1, var2_ready, rstd2_ready, B - 1)
            low(1)
            pool.wait_ge(pool_step, 4)
            gate_exp(0)
            for n in range(2, UNITS):
                if n == 3:
                    rstd_of(1, var2_ready, rstd2_ready, B)
                if n == 10:
                    gate_exp(1)
                if n not in LOW_ON_DVE:
                    low(n)

        @block.scalar
        def _(act):
            def take(s):
                act.wait_ge(filled, place[s] + 1)

            def copy(dst, src, s):
                nc.scalar.activation(dst, src, ACT.Copy).then_inc(act_took, 1)

            def take_xn1T(b):
                s = ("xn1T", b)
                take(s)
                copy(xn1T[:, :], bank(s)[:, 0:S], s)

            def take_q(b):
                s = ("q", b)
                take(s)
                if b >= 1:
                    act.wait_ge(q_split, b)
                nc.scalar.activation(q_f[:, :], bank(s)[:, 0:S], ACT.Identity, bias=q_bias[:, 0:1], scale=SCALE)
                nc.scalar.activation(q_hi[:, b % 2, :], bank(s)[:, 0:S], ACT.Identity, bias=q_bias[:, 0:1],
                                     scale=SCALE).then_inc(act_took, 1)

            def take_ctxT(b, g):
                s = ("ctxT", b, g)
                take(s)
                lo, hi = 4 * g * P, min(4 * (g + 1) * P, KC)
                copy(ctxT_hi[:, b % 2, lo:hi], bank(s)[:, 0:hi - lo], s)

            def take_probsT(t, g):
                s = ("probsT", t, g)
                take(s)
                b, j = t // NJ, t % NJ
                n, rows = len(group_chunks(g)), chunk_rows(4 * g)
                copy(probsT[0:rows, b % 2, 4 * g:4 * g + n, j * P:(j + 1) * P],
                     bank(s)[0:rows, 0:n * P].rearrange("p (c q) -> p c q", q=P), s)

            def exps(t):
                act.wait_ge(max_ready, t + 1)
                if t >= 2:
                    act.wait_ge(filled, place[("probsT", t - 2, NG - 1)] + 1)
                for h, (lo, hi) in enumerate(((0, SPLIT_A), (SPLIT_A, KC))):
                    nc.scalar.activation(probs[:, t % 2, lo:hi], scores[:, lo:hi], ACT.Exp, bias=neg_max[:, t:t + 1],
                                         accum_out=exp_sum[:, t, h:h + 1]).then_inc(exped, 1)

            def take_pc(b):
                act.wait_ge(pv_done, b + 1)
                if b >= 1:
                    act.wait_ge(filled, place[("attn", b - 1)] + 1)
                nc.scalar.activation(pcT[:, :], acc[b % 2][:, 0:S], ACT.Copy).then_inc(pc_copied, 1)

            def take_xn2T(b):
                s = ("xn2T", b)
                take(s)
                copy(xn2T_hi[:, b * S:(b + 1) * S], bank(s)[:, 0:S], s)

            def take_gate(half, e):
                s = ("gate", half, e)
                take(s)
                if half:
                    act.wait_ge(y_taken, e + 1)
                copy(gate_rows[:, e, :], bank(s)[:, 0:HT], s)

            nc.scalar.preload_act_table(ACT.Exp)
            take(("qk_w",))
            qk = bank(("qk_w",))
            nc.scalar.activation(q_bias[:, :], qk[:, D:D + 1], ACT.Copy, scale=SCALE)
            nc.scalar.activation(qk_w[:, :], qk[:, 0:D], ACT.Copy).then_inc(act_took, 1)
            take_xn1T(0)
            take_q(0)
            for g in range(NG):
                take_ctxT(0, g)
            for s, dst in ((("woT",), woT), (("vo_w",), vo_w), (("out_bias",), out_bias)):
                take(s)
                copy(dst[:, :], bank(s)[:, 0:D], s)

            for b in range(B):
                if b >= 1:
                    for g in range(NG):
                        take_probsT(2 * b - 1, g)
                if b + 1 < B:
                    take_ctxT(b + 1, 0)
                    take_ctxT(b + 1, 1)
                exps(2 * b)
                for g in range(NG):
                    take_probsT(2 * b, g)
                if b + 1 < B:
                    take_xn1T(b + 1)
                    take_ctxT(b + 1, 2)
                exps(2 * b + 1)
                if b + 1 < B:
                    take_ctxT(b + 1, 3)
                    take_q(b + 1)
                if b >= 1:
                    take_pc(b - 1)
                if b >= 2:
                    take_xn2T(b - 2)

            def silu(n):
                act.wait_ge(a_done, n + 1)
                if n >= 2:
                    act.wait_ge(h_done, n - 1)
                nc.scalar.activation(act_a[:, n % 2, :], a_ps[n % 2], ACT.Silu).then_inc(silu_done, 1)

            def high(n):
                act.wait_ge(h_done, n + 1)
                if n >= 3:
                    act.wait_ge(y_done, n - 2)
                nc.scalar.activation(h_hi[:, n % 3, :], h_f[:, n % 3, :], ACT.Copy).then_inc(hh_done, 1)

            for g in range(NG):
                take_probsT(NT - 1, g)
            silu(0)
            silu(1)
            high(0)
            high(1)
            take_pc(B - 1)
            take_xn2T(B - 2)
            for n in range(2, UNITS):
                silu(n)
                for s in late.get(n, ()):
                    if s[0] == "gate":
                        take_gate(s[1], s[2])
                    if s[0] == "xn2T":
                        take_xn2T(s[1])
                high(n)

        @block.vector
        def _(dve):
            steps = [0]

            def then(ins):
                steps[0] += 1
                ins.then_inc(dve_step, 1)
                dve.wait_ge(dve_step, steps[0])

            def norm_stats(ln, tiles, sem_out):
                for j in range(NJ):
                    nc.vector.bn_stats(stats[:, ln, j, :], tiles[:, j, :]).then_inc(dve_step, 1)
                steps[0] += NJ
                dve.wait_ge(dve_step, steps[0])
                for j in range(NJ):
                    nc.vector.bn_aggr(mean_var[:, ln, j, :], stats[:, ln, j, :]).then_inc(dve_step, 1)
                steps[0] += NJ
                dve.wait_ge(dve_step, steps[0])
                nc.vector.tensor_scalar(var_eps[:, ln, :], mean_var[:, ln, :, 1], EPS, None, ALU.add).then_inc(sem_out, 1)

            def normalise(ln, dst, tiles, sem_in, count, sem_out):
                dve.wait_ge(sem_in, count)
                for j in range(NJ):
                    nc.vector.tensor_scalar(dst[:, j, :], tiles[:, j, :], mean_var[:, ln, j, 0:1],
                                            rstd[:, ln, j:j + 1], ALU.subtract, ALU.mult).then_inc(sem_out, 1)

            def ln1_stats(b):
                dve.wait_ge(x0_loaded if b == 0 else x_loaded, 16)
                norm_stats(0, x_sb[:, NJ * b:NJ * (b + 1), :], var1_ready)

            def ln1(b):
                if b >= 1:
                    dve.wait_ge(filled, place[("xn1T", b - 1)] + 1)
                normalise(0, xn1, x_sb[:, NJ * b:NJ * (b + 1), :], rstd1_ready, b + 1, xn1_ready)

            def maxima(t):
                for h, (lo, hi) in enumerate(((0, SPLIT_A), (SPLIT_A, KC))):
                    dve.wait_ge(scored, 2 * t + h + 1)
                    nc.vector.tensor_reduce(row_max[:, t, h:h + 1], scores[:, lo:hi], AXX, ALU.max).then_inc(dve_step, 1)
                steps[0] += 2
                dve.wait_ge(dve_step, steps[0])
                nc.vector.tensor_reduce(neg_max[:, t:t + 1], row_max[:, t, :], AXX, ALU.max,
                                        negate=True).then_inc(max_ready, 1)

            def denominators(b):
                dve.wait_ge(exped, 4 * (b + 1))
                t = slice(NJ * b, NJ * (b + 1))
                then(nc.vector.tensor_tensor(denom[:, t], exp_sum[:, t, 0], exp_sum[:, t, 1], ALU.add))
                then(nc.vector.reciprocal(rdenom[:, t], denom[:, t]))

            def ctxT_low(b, g):
                s = ("ctxT", b, g)
                dve.wait_ge(act_took, takes(s, "A"))
                lo, hi = 4 * g * P, min(4 * (g + 1) * P, KC)
                nc.vector.tensor_tensor(ctxT_lo[:, b % 2, lo:hi], bank(s)[:, 0:hi - lo],
                                        ctxT_hi[:, b % 2, lo:hi].bitcast(F32), ALU.subtract).then_inc(dve_took, 1)

            def q_low(b):
                dve.wait_ge(act_took, takes(("q", b), "A"))
                nc.vector.tensor_tensor(q_lo[:, b % 2, :], q_f[:, :], q_hi[:, b % 2, :].bitcast(F32),
                                        ALU.subtract).then_inc(q_split, 1)

            def weight_high(k):
                e, which = k // 3, k % 3
                dve.wait_ge(raw_loaded[k % RAW], 16 * (k // RAW + 1))
                nc.vector.tensor_copy(w_hi[:, e, which, :], w_raw[:, k % RAW, :]).then_inc(wh_ready, 1)

            def residual(b):
                s = ("attn", b)
                if b == 0:
                    dve.wait_ge(xbias_ready, 1)
                denominators(b)
                dve.wait_ge(filled, place[s] + 1)
                for j in range(NJ):
                    t = NJ * b + j
                    ins = nc.vector.scalar_tensor_tensor(x2[:, t, :], bank(s)[:, j * P:(j + 1) * P], rdenom[:, t:t + 1],
                                                         x_bias[:, t, :], ALU.mult, ALU.add)
                    if j == NJ - 1:
                        ins.then_inc(dve_took, 1)
                dve.wait_ge(dve_took, takes(s, "D"))
                norm_stats(1, x2[:, NJ * b:NJ * (b + 1), :], var2_ready)

            def ln2(b):
                if b >= 1:
                    dve.wait_ge(filled, place[("xn2T", b - 1)] + 1)
                normalise(1, xn2, x2[:, NJ * b:NJ * (b + 1), :], rstd2_ready, b + 1, xn2_ready)

            def xn2T_low(b):
                s = ("xn2T", b)
                dve.wait_ge(act_took, takes(s, "A"))
                c = slice(b * S, (b + 1) * S)
                nc.vector.tensor_tensor(xn2T_lo[:, c], bank(s)[:, 0:S], xn2T_hi[:, c].bitcast(F32),
                                        ALU.subtract).then_inc(dve_took, 1)

            def take_logits(b):
                s = ("logits", b)
                dve.wait_ge(filled, place[s] + 1)
                nc.vector.tensor_tensor(logits[:, NJ * b:NJ * (b + 1), :],
                                        bank(s)[:, 0:NJ * E].rearrange("p (j e) -> p j e", e=E),
                                        rb_sb[:, :].rearrange("p (o e) -> p o e", o=1).broadcast_to([P, NJ, E]),
                                        ALU.add).then_inc(dve_took, 1)
                dve.wait_ge(dve_took, takes(s, "D"))

            def rank_experts(half):
                lg = logits[:, half * TPH:(half + 1) * TPH, :]
                as_j = lg.rearrange("p t (o j) -> p t o j", o=1).broadcast_to([P, TPH, E, E])
                as_e = lg.rearrange("p t (e o) -> p t e o", o=1).broadcast_to([P, TPH, E, E])
                then(nc.vector.tensor_reduce(top[:, :], lg, AXX, ALU.max))
                nc.vector.tensor_tensor(shifted[:, :, :], lg,
                                        top[:, :].rearrange("p (t o) -> p t o", o=1).broadcast_to([P, TPH, E]),
                                        ALU.subtract).then_inc(shift_ready, 1)
                nc.vector.tensor_tensor(greater[:, :, :, :], as_j, as_e, ALU.is_gt)
                then(nc.vector.tensor_tensor(equal[:, :, :, :], as_j, as_e, ALU.is_equal))
                then(nc.vector.tensor_tensor(equal[:, :, :, :], equal[:, :, :, :],
                                             below[:, :, :].rearrange("p (o e) j -> p o e j", o=1)
                                             .broadcast_to([P, TPH, E, E]), ALU.mult))
                then(nc.vector.tensor_tensor(beaten[:, :, :, :], greater[:, :, :, :], equal[:, :, :, :], ALU.add))
                then(nc.vector.tensor_reduce(rank[:, :, :], beaten[:, :, :, :], AXX, ALU.add))

            def make_gates(half):
                dve.wait_ge(ex_ready, half + 1)
                then(nc.vector.scalar_tensor_tensor(kept[:, :, :], rank[:, :, :], 1.5, ex[:, :, :], ALU.is_lt, ALU.mult))
                then(nc.vector.tensor_reduce(kept_sum[:, :], kept[:, :, :], AXX, ALU.add))
                then(nc.vector.reciprocal(rkept[:, :], kept_sum[:, :]))
                nc.vector.tensor_tensor(gates[:, :, :], kept[:, :, :],
                                        rkept[:, :].rearrange("p (t o) -> p t o", o=1).broadcast_to([P, TPH, E]),
                                        ALU.mult).then_inc(gates_ready, 1)

            if KPAD > KC:
                nc.vector.memset(ctxT_hi[:, :, KC:KPAD].bitcast(F32), 0.0).then_inc(consts_ready, 1)
                nc.vector.memset(ctxT_lo[:, :, KC:KPAD].bitcast(F32), 0.0).then_inc(consts_ready, 1)
            ln1_stats(0)
            ln1(0)
            q_low(0)
            for g in range(NG):
                ctxT_low(0, g)
            dve.wait_ge(small_loaded, 32)
            then(nc.vector.tensor_copy(rw_hi[:, :], rw_sb[:, :]))
            then(nc.vector.tensor_tensor(rw_lo[:, :], rw_sb[:, :], rw_hi[:, :].bitcast(F32), ALU.subtract))
            dve.wait_ge(consts_ready, 5)

            for b in range(B):
                if b + 1 < B:
                    ln1_stats(b + 1)
                maxima(2 * b)
                if b + 1 < B:
                    ctxT_low(b + 1, 0)
                    ctxT_low(b + 1, 1)
                if b >= 2:
                    residual(b - 2)
                if b >= 3:
                    take_logits(b - 3)
                if b + 1 < B:
                    ln1(b + 1)
                if b >= 2:
                    ln2(b - 2)
                maxima(2 * b + 1)
                if b + 1 < B:
                    ctxT_low(b + 1, 2)
                for k in range(3 * b, 3 * b + 3):
                    weight_high(k)
                if b + 1 < B:
                    ctxT_low(b + 1, 3)
                    q_low(b + 1)
                if b >= 2:
                    xn2T_low(b - 2)

            def combine(k):
                half, e = k // E, k % E
                dve.wait_ge(y_done, FC * (k + 1))
                dve.wait_ge(act_took, takes(("gate", half, e), "A"))
                ins = nc.vector.tensor_tensor(moeT[:, :] if e == 0 else gated[:, k % 2, :],
                                              acc[k % 2][:, 0:HT], gate_rows[:, e, :], ALU.mult)
                ins.then_inc(y_taken, 1)
                if e:
                    dve.wait_ge(y_taken, k + 1)
                    ins = nc.vector.tensor_tensor(moeT[:, :], moeT[:, :], gated[:, k % 2, :], ALU.add)
                    if e == E - 1:
                        ins.then_inc(moe_ready, 1)
                    else:
                        then(ins)

            def finish(half):
                s = ("outT", half)
                dve.wait_ge(filled, place[s] + 1)
                t = slice(half * TPH, (half + 1) * TPH)
                nc.vector.tensor_tensor(y_sb[:, t, :], bank(s)[:, 0:HT].rearrange("p (t d) -> p t d", d=D),
                                        x2[:, t, :], ALU.add).then_inc(dve_took, 1)

            def product(n):
                dve.wait_ge(silu_done, n + 1)
                dve.wait_ge(b_done, n + 1)
                if n >= 3:
                    dve.wait_ge(hl_dve if n - 3 in LOW_ON_DVE else hl_done, lows(n - 3))
                nc.vector.tensor_tensor(h_f[:, n % 3, :], b_ps[n % 2], act_a[:, n % 2, :], ALU.mult).then_inc(h_done, 1)

            def low(n):
                dve.wait_ge(hh_done, n + 1)
                dve.wait_ge(y_done, n - 2)
                nc.vector.tensor_tensor(h_lo[:, n % 3, :], h_f[:, n % 3, :], h_hi[:, n % 3, :].bitcast(F32),
                                        ALU.subtract).then_inc(hl_dve, 1)

            product(0)
            residual(B - 2)
            product(1)
            take_logits(1)
            rank_experts(0)
            ln2(B - 2)
            make_gates(0)
            xn2T_low(B - 2)
            for n in range(2, UNITS):
                product(n)
                if n in LOW_ON_DVE:
                    low(n)
                if n == 2:
                    take_logits(2)
                    residual(3)
                if n == 3:
                    ln2(3)
                if n == 5:
                    xn2T_low(3)
                if n == 8:
                    take_logits(3)
                    rank_experts(1)
                if n == 11:
                    make_gates(1)
                if n >= 6 and n % FC == 2:
                    combine((n - 6) // FC)
                if n == 21:
                    finish(0)
            combine(2 * E - 1)
            finish(1)

        @block.tensor
        def _(pe):
            def open_slot(s):
                n = before(place[s])
                if n is not None:
                    emptied(slots[n])

            def emptied(old):
                if READERS[old[0]].endswith("D"):
                    pe.wait_ge(dve_took, takes(old, "D"))
                else:
                    pe.wait_ge(act_took, takes(old, "A"))

            def matmul3(dst, lhs_hi, lhs_lo, rhs_hi, rhs_lo, first=True, last=True):
                nc.tensor.matmul(dst, lhs_hi, rhs_hi, start=first, stop=False)
                nc.tensor.matmul(dst, lhs_hi, rhs_lo, start=False, stop=False)
                return nc.tensor.matmul(dst, lhs_lo, rhs_hi, start=False, stop=last)

            def fill_xn1T(b):
                s = ("xn1T", b)
                open_slot(s)
                pe.wait_ge(xn1_ready, NJ * (b + 1))
                for j in range(NJ):
                    ins = nc.tensor.transpose(bank(s)[:, j * P:(j + 1) * P], xn1[:, j, :], ident[:, :])
                ins.then_inc(filled, 1)

            def fill_q(b):
                s = ("q", b)
                open_slot(s)
                pe.wait_ge(act_took, takes(("xn1T", b), "A"))
                nc.tensor.matmul(bank(s)[:, 0:S], qk_w[:, :], xn1T[:, :], start=True, stop=True).then_inc(filled, 1)

            def fill_ctxT(b, g):
                s = ("ctxT", b, g)
                open_slot(s)
                if g in (0, 2):
                    pe.wait_ge(ctx_loaded[b][g // 2], (16, 32)[g // 2])
                for i, c in enumerate(group_chunks(g)):
                    r = chunk_rows(c)
                    ins = nc.tensor.transpose(bank(s)[:, i * P:i * P + r], ctx_sb[0:r, b, c, :], ident[0:r, 0:r])
                ins.then_inc(filled, 1)

            def fill_probsT(t, g):
                s = ("probsT", t, g)
                open_slot(s)
                pe.wait_ge(exped, 2 * t + (1 if 4 * (g + 1) * P <= SPLIT_A else 2))
                for i, c in enumerate(group_chunks(g)):
                    r = chunk_rows(c)
                    ins = nc.tensor.transpose(bank(s)[0:r, i * P:(i + 1) * P],
                                              probs[:, t % 2, c * P:c * P + r], ident[:, :])
                ins.then_inc(filled, 1)

            def score(t, h):
                b, j = t // NJ, t % NJ
                if j == 0:
                    pe.wait_ge(q_split, b + 1)
                    pe.wait_ge(dve_took, takes(("ctxT", b, (1, NG - 1)[h]), "D"))
                if t >= 1:
                    pe.wait_ge(exped, 2 * t - 1 + h)
                lo, end = (0, SPLIT_A) if h == 0 else (SPLIT_A, KPAD)
                q = slice(j * P, (j + 1) * P)
                pieces = [(c, min(c + BANK, end)) for c in range(lo, end, BANK)]
                hi, low = q_hi[:, b % 2, q], q_lo[:, b % 2, q]
                for c0, c1 in pieces:
                    nc.tensor.matmul(scores[:, c0:c1], hi, ctxT_hi[:, b % 2, c0:c1], start=True, stop=False)
                    nc.tensor.matmul(scores[:, c0:c1], hi, ctxT_lo[:, b % 2, c0:c1], start=False, stop=False)
                for c0, c1 in pieces:
                    ins = nc.tensor.matmul(scores[:, c0:c1], low, ctxT_hi[:, b % 2, c0:c1], start=False, stop=True)
                ins.then_inc(scored, 1)

            def values(b, first, end):
                if first == 0:
                    pe.wait_ge(act_took, takes(("probsT", NJ * b + 1, NG - 1), "A"))
                    if b >= 2:
                        pe.wait_ge(pc_copied, b - 1)
                    else:
                        emptied(slots[max(n for n in range(len(slots)) if ring[n] == 4 and banks[n] == 2 + b)])
                for c in range(first, end):
                    r = chunk_rows(c)
                    ins = nc.tensor.matmul(acc[b % 2][:, 0:S], ctx_sb[0:r, b, c, :], probsT[0:r, b % 2, c, :],
                                           start=(c == 0), stop=(c == NCH - 1))
                if end == NCH:
                    ins.then_inc(pv_done, 1)

            def fill_attn(b):
                s = ("attn", b)
                open_slot(s)
                pe.wait_ge(pc_copied, b + 1)
                for j in range(NJ):
                    ins = nc.tensor.matmul(bank(s)[:, j * P:(j + 1) * P], pcT[:, j * P:(j + 1) * P], vo_w[:, :],
                                           start=True, stop=True)
                ins.then_inc(filled, 1)

            def fill_xn2T(b):
                s = ("xn2T", b)
                open_slot(s)
                pe.wait_ge(xn2_ready, NJ * (b + 1))
                for j in range(NJ):
                    ins = nc.tensor.transpose(bank(s)[:, j * P:(j + 1) * P], xn2[:, j, :], ident[:, :])
                ins.then_inc(filled, 1)

            def fill_logits(b):
                s = ("logits", b)
                open_slot(s)
                pe.wait_ge(dve_took, takes(("xn2T", b), "D"))
                for j in range(NJ):
                    q = slice(b * S + j * P, b * S + (j + 1) * P)
                    ins = matmul3(bank(s)[:, j * E:(j + 1) * E], xn2T_hi[:, q], xn2T_lo[:, q], rw_hi[:, :], rw_lo[:, :])
                ins.then_inc(filled, 1)

            def fill_gate(half, e):
                s = ("gate", half, e)
                open_slot(s)
                pe.wait_ge(gates_ready, half + 1)
                for t in range(TPH):
                    ins = nc.tensor.transpose(bank(s)[:, t * P:(t + 1) * P],
                                              gates[:, t, e:e + 1].broadcast_to([P, P]), ident[:, :])
                ins.then_inc(filled, 1)

            def fill_outT(half):
                s = ("outT", half)
                open_slot(s)
                pe.wait_ge(moe_ready, half + 1)
                for t in range(TPH):
                    ins = nc.tensor.transpose(bank(s)[:, t * P:(t + 1) * P], moeT[:, t * P:(t + 1) * P], ident[:, :])
                ins.then_inc(filled, 1)

            FILL = {"logits": fill_logits, "attn": fill_attn, "gate": fill_gate, "xn2T": fill_xn2T, "outT": fill_outT}

            def fill_product(s, *pairs):
                open_slot(s)
                for i, (lhsT, rhs) in enumerate(pairs):
                    ins = nc.tensor.matmul(bank(s)[:, 0:D], lhsT, rhs, start=(i == 0), stop=(i == len(pairs) - 1))
                ins.then_inc(filled, 1)

            pe.wait_ge(wqk_loaded, 48)
            qk = bank(("qk_w",))
            nc.tensor.matmul(qk[:, 0:D], wq_sb[:, :], wk_sb[:, :], start=True, stop=True)
            nc.tensor.matmul(qk[:, D:D + 1], wk_sb[:, :], bq_sb[:, :], start=True, stop=True).then_inc(filled, 1)
            pe.wait_ge(consts_ready, 1)
            fill_xn1T(0)
            fill_q(0)
            for g in range(NG):
                fill_ctxT(0, g)

            def output_weights():
                pe.wait_ge(wvo_loaded, 64)
                open_slot(("woT",))
                nc.tensor.transpose(bank(("woT",))[:, 0:D], wo_sb[:, :], ident[:, :]).then_inc(filled, 1)
                pe.wait_ge(act_took, takes(("woT",), "A"))
                fill_product(("vo_w",), (wv_sb[:, :], woT[:, :]))
                pe.wait_ge(consts_ready, 5)
                fill_product(("out_bias",), (bv_sb[:, 0:1].broadcast_to([P, P]), woT[:, :]), (ones_row[:, :], bo_sb[:, :]))

            def expert_a(n):
                half, e, c = unit(n)
                tok = slice(half * HT, (half + 1) * HT)
                f = slice(c * P, (c + 1) * P)
                if n % FC == 0 and half == 0:
                    pe.wait_ge(wl_ready, 3 * (e + 1))
                if n % (E * FC) == 0:
                    pe.wait_ge(dve_took, takes(("xn2T", BPH * (half + 1) - 1), "D"))
                if n >= 2:
                    pe.wait_ge(silu_done, n - 1)
                else:
                    pe.wait_ge(exped, 2 * NT - 1)
                matmul3(a_ps[n % 2], w_hi[:, e, 0, f], w_lo[:, e, 0, f], xn2T_hi[:, tok], xn2T_lo[:, tok]).then_inc(a_done, 1)

            def expert_b(n):
                half, e, c = unit(n)
                tok = slice(half * HT, (half + 1) * HT)
                f = slice(c * P, (c + 1) * P)
                if n >= 2:
                    pe.wait_ge(h_done, n - 1)
                else:
                    pe.wait_ge(exped, 2 * NT)
                matmul3(b_ps[n % 2], w_hi[:, e, 1, f], w_lo[:, e, 1, f], xn2T_hi[:, tok], xn2T_lo[:, tok]).then_inc(b_done, 1)

            def expert_out(n):
                half, e, c = unit(n)
                k = n // FC
                if c == 0 and k >= 2:
                    pe.wait_ge(y_taken, k - 1)
                if k < 2 and c == 0:
                    pe.wait_ge(pc_copied, B - 1 + k)
                pe.wait_ge(hl_dve if n in LOW_ON_DVE else hl_done, lows(n))
                d = slice(c * D, (c + 1) * D)
                matmul3(acc[k % 2][:, 0:HT], w_hi[:, e, 2, d], w_lo[:, e, 2, d], h_hi[:, n % 3, :], h_lo[:, n % 3, :],
                        first=(c == 0), last=(c == FC - 1)).then_inc(y_done, 1)

            def value_run(b, *cuts):
                if b >= 0:
                    values(b, *cuts)

            for b in range(B):
                v = b - 1
                nxt = b + 1 < B
                if b >= 1:
                    fill_probsT(2 * b - 1, 0)
                    fill_probsT(2 * b - 1, 1)
                score(2 * b, 0)
                if b >= 1:
                    fill_probsT(2 * b - 1, 2)
                    fill_probsT(2 * b - 1, 3)
                score(2 * b, 1)
                if b == 0:
                    output_weights()
                if nxt:
                    fill_ctxT(b + 1, 0)
                value_run(v, 0, 1)
                if nxt:
                    fill_ctxT(b + 1, 1)
                value_run(v, 1, 2)
                if b >= 2:
                    fill_attn(b - 2)
                value_run(v, 2, 4)
                if b >= 3:
                    fill_logits(b - 3)
                value_run(v, 4, 6)
                fill_probsT(2 * b, 0)
                fill_probsT(2 * b, 1)
                score(2 * b + 1, 0)
                fill_probsT(2 * b, 2)
                fill_probsT(2 * b, 3)
                score(2 * b + 1, 1)
                if nxt:
                    fill_xn1T(b + 1)
                value_run(v, 6, 7)
                if nxt:
                    fill_ctxT(b + 1, 2)
                value_run(v, 7, 8)
                if nxt:
                    fill_ctxT(b + 1, 3)
                value_run(v, 8, 10)
                if nxt:
                    fill_q(b + 1)
                value_run(v, 10, 13)
                if b >= 2:
                    fill_xn2T(b - 2)

            fill_probsT(NT - 1, 0)
            fill_probsT(NT - 1, 1)
            expert_a(0)
            fill_probsT(NT - 1, 2)
            fill_probsT(NT - 1, 3)
            expert_b(0)
            fill_attn(B - 2)
            expert_a(1)
            fill_logits(B - 3)
            expert_b(1)
            values(B - 1, 0, NCH)
            fill_xn2T(B - 2)
            expert_out(0)
            for n in range(2, UNITS):
                expert_a(n)
                expert_b(n)
                if n >= 3:
                    expert_out(n - 2)
                for s in late.get(n, ()):
                    FILL[s[0]](*s[1:])
            expert_out(UNITS - 2)
            expert_out(UNITS - 1)
            for s in late[UNITS]:
                FILL[s[0]](*s[1:])


_INS = ["x", "ctx_1024", "L0_xattn_Wk", "L0_xattn_Wv", "L0_xattn_bv", "L0_xattn_Wq", "L0_xattn_bq", "L0_xattn_Wo",
        "L0_xattn_bo", "L0_ffn_router_w", "L0_ffn_router_b", "L0_ffn_w1", "L0_ffn_w3", "L0_ffn_w2"]


def kernel(**inputs):
    import numpy as np
    import concourse.bacc as bacc
    from concourse import mybir as mb
    from concourse.bass_utils import run_bass_kernel_spmd as run

    nc = bacc.Bacc("TRN2", target_bir_lowering=False, num_devices=1)
    arrays, args = {}, []
    for name in _INS:
        a = np.ascontiguousarray(inputs[name])
        arrays[f"in_{name}_dram"] = a
        args.append(nc.dram_tensor(f"in_{name}_dram", a.shape, mb.dt.from_np(a.dtype), kind="ExternalInput").ap())
    shape = inputs["x"].shape
    out = nc.dram_tensor("out_dram", shape, mb.dt.float32, kind="ExternalOutput").ap()
    xattn_moe_program(nc, *args, out)
    r = run(nc, [arrays], core_ids=[0])
    return r.results[0]["out_dram"]
```

```python
import concourse.bass as bass
from concourse import mybir
from contextlib import ExitStack

F32 = mybir.dt.float32
F32R = mybir.dt.float32r
ALU = mybir.AluOpType
ACT = mybir.ActivationFunctionType
AXX = mybir.AxisListType.X


def xattn_moe_program(nc, x, ctx, wk, wv, bv, wq, bq, wo, bo, rw, rb, w1, w3, w2, out):
    B, S, D = x.shape
    KC = ctx.shape[1]
    E, _, F = w1.shape
    P = 128
    NJ = S // P
    NT = B * NJ
    FULL = KC // P
    TAIL = KC - FULL * P
    NCH = FULL + 1
    KPAD = KC + KC % 2
    SPLIT_G = 2
    SPLIT_C = 4 * SPLIT_G
    NG = -(-NCH // 4)
    HALVES = 2
    HT = NT // HALVES * P
    TPH = HT // P
    BPH = B // HALVES
    FC = F // P
    UNITS = HALVES * E * FC
    BANK = 512
    SPLIT_A = 2 * BANK
    LOW_ON_DVE = (11, 12, 30, 31)
    WARM = 8
    EPS = 1e-5
    SCALE = 1.0 / float(D) ** 0.5

    def group_chunks(g):
        return range(4 * g, min(4 * g + 4, NCH))

    def chunk_rows(c):
        return P if c < FULL else TAIL

    stack = ExitStack()
    with stack:
        def sb(name, shape, dt=F32):
            return stack.enter_context(nc.sbuf_tensor(name, shape, dt))

        def ps(name, cols):
            return stack.enter_context(nc.psum_tensor(name, [P, cols], F32))

        def sem(name):
            return stack.enter_context(nc.semaphore(name))

        x_sb = sb("x_sb", [P, NT, D])
        x_bias = sb("x_bias", [P, NT, D])
        x2 = sb("x2", [P, NT, D])
        xn1 = sb("xn1", [P, NJ, D])
        xn2 = sb("xn2", [P, NJ, D])
        ctx_sb = sb("ctx_sb", [P, B, NCH, D])
        ctxT_hi = sb("ctxT_hi", [P, 2, KPAD], F32R)
        ctxT_lo = sb("ctxT_lo", [P, 2, KPAD], F32R)
        probs = sb("probs", [P, 2, KPAD])
        probsT_hi = sb("probsT_hi", [P, 2, SPLIT_C, S], F32R)
        probsT_lo = sb("probsT_lo", [P, 2, SPLIT_C, S], F32R)
        probsT = sb("probsT", [P, 2, NCH - SPLIT_C, S])
        ctx_hi = sb("ctx_hi", [P, SPLIT_C, D], F32R)
        ctx_lo = sb("ctx_lo", [P, SPLIT_C, D], F32R)
        xn1T = sb("xn1T", [P, S])
        q_f = sb("q_f", [P, S])
        q_hi = sb("q_hi", [P, 2, S], F32R)
        q_lo = sb("q_lo", [P, 2, S], F32R)
        pcT = sb("pcT", [P, S])
        xn2T_hi = sb("xn2T_hi", [P, NT * P], F32R)
        xn2T_lo = sb("xn2T_lo", [P, NT * P], F32R)
        ident = sb("ident", [P, P])
        ones_row = sb("ones_row", [1, P])
        wq_sb = sb("wq_sb", [P, D])
        wk_sb = sb("wk_sb", [P, D])
        wv_sb = sb("wv_sb", [P, D])
        wo_sb = sb("wo_sb", [P, D])
        woT = sb("woT", [P, D])
        qk_w = sb("qk_w", [P, D])
        vo_w = sb("vo_w", [P, D])
        q_bias = sb("q_bias", [P, 1])
        out_bias = sb("out_bias", [P, D])
        bq_sb = sb("bq_sb", [P, 1])
        bv_sb = sb("bv_sb", [P, 1])
        bo_sb = sb("bo_sb", [1, D])
        rw_sb = sb("rw_sb", [P, E])
        rw_hi = sb("rw_hi", [P, E], F32R)
        rw_lo = sb("rw_lo", [P, E], F32R)
        rb_sb = sb("rb_sb", [P, E])
        row_max = sb("row_max", [P, NT, 2])
        neg_max = sb("neg_max", [P, NT])
        exp_sum = sb("exp_sum", [P, NT, 2])
        denom = sb("denom", [P, NT])
        rdenom = sb("rdenom", [P, NT])
        stats = sb("stats", [P, 2, NJ, 6])
        mean_var = sb("mean_var", [P, 2, NJ, 2])
        var_eps = sb("var_eps", [P, 2, NJ])
        rstd = sb("rstd", [P, 2, NJ])
        neg_half = sb("neg_half", [P, NJ])
        euler = sb("euler", [P, TPH * E])
        below = sb("below", [P, E, E])
        logits = sb("logits", [P, NT, E])
        top = sb("top", [P, TPH])
        shifted = sb("shifted", [P, TPH, E])
        ex = sb("ex", [P, TPH, E])
        greater = sb("greater", [P, TPH, E, E])
        equal = sb("equal", [P, TPH, E, E])
        beaten = sb("beaten", [P, TPH, E, E])
        rank = sb("rank", [P, TPH, E])
        kept = sb("kept", [P, TPH, E])
        kept_sum = sb("kept_sum", [P, TPH])
        rkept = sb("rkept", [P, TPH])
        gates = sb("gates", [P, E, TPH])
        gatesT = sb("gatesT", [TPH * E, HALVES, P])
        RAW = 4
        w_raw = sb("w_raw", [P, RAW, F])
        w_hi = sb("w_hi", [P, E, 3, F], F32R)
        w_lo = sb("w_lo", [P, E, 3, F], F32R)
        gate_rows = ctx_sb[:, :, :, :].rearrange("p b c d -> p (b c d)")[:, 0:HALVES * E * HT] \
            .rearrange("p (h e t) -> p h e t", h=HALVES, e=E)
        gates_dram = nc.dram_tensor("gates_scratch", (HALVES, E, TPH, P), F32, kind="Internal").ap()
        act_a = probs[:, 0, 0:2 * HT].rearrange("p (n t) -> p n t", t=HT)
        gated = probs[:, 1, 0:2 * HT].rearrange("p (n t) -> p n t", t=HT)
        h_hi = probsT_hi[:, 0, :, :].rearrange("p c q -> p (c q)")[:, 0:3 * HT].rearrange("p (n t) -> p n t", t=HT)
        h_lo = probsT_lo[:, 0, :, :].rearrange("p c q -> p (c q)")[:, 0:3 * HT].rearrange("p (n t) -> p n t", t=HT)
        past_gates = HALVES * E * HT
        h_f = [ctx_sb[:, :, :, :].rearrange("p b c d -> p (b c d)")[:, past_gates:past_gates + HT],
               probs[:, 0, 2 * HT:3 * HT], probs[:, 1, 2 * HT:3 * HT]]
        moeT = probsT[:, 0, :, :].rearrange("p c q -> p (c q)")[:, 0:HT]
        y_sb = x_sb

        scores = ps("scores", 2048)
        transit = [ps("transit0", 512), ps("transit1", 512)]
        acc = [ps("acc0", 512), ps("acc1", 512)]
        a_ps = [scores[:, 0:HT], scores[:, 512:512 + HT]]
        b_ps = [scores[:, 1024:1024 + HT], scores[:, 1536:1536 + HT]]

        x0_loaded, x_loaded = sem("x0_loaded"), sem("x_loaded")
        wqk_loaded, wvo_loaded, small_loaded = sem("wqk_loaded"), sem("wvo_loaded"), sem("small_loaded")
        ctx_loaded = [(sem(f"ctx_first{b}"), sem(f"ctx_rest{b}")) for b in range(B)]
        raw_loaded = [sem(f"raw_loaded{r}") for r in range(RAW)]
        gates_out = sem("gates_out")
        rows_loaded = [sem(f"rows_loaded{h}") for h in range(HALVES)]
        stored = sem("stored")
        consts_ready = sem("consts_ready")
        pool_step = sem("pool_step")
        zeros_ready = sem("zeros_ready")
        filled = sem("filled")
        act_took = sem("act_took")
        dve_took = sem("dve_took")
        scored = sem("scored")
        max_ready = sem("max_ready")
        exped = sem("exped")
        pv_done = sem("pv_done")
        pc_copied = sem("pc_copied")
        q_split = sem("q_split")
        var1_ready, rstd1_ready, xn1_ready = sem("var1_ready"), sem("rstd1_ready"), sem("xn1_ready")
        var2_ready, rstd2_ready, xn2_ready = sem("var2_ready"), sem("rstd2_ready"), sem("xn2_ready")
        xbias_ready = sem("xbias_ready")
        shift_ready, ex_ready, gates_ready = sem("shift_ready"), sem("ex_ready"), sem("gates_ready")
        wh_ready, wl_ready = sem("wh_ready"), sem("wl_ready")
        a_done, b_done, y_done = sem("a_done"), sem("b_done"), sem("y_done")
        silu_done, h_done, hh_done, hl_done = sem("silu_done"), sem("h_done"), sem("hh_done"), sem("hl_done")
        hl_dve = sem("hl_dve")
        ctx_high, ctx_low = sem("ctx_high"), sem("ctx_low")
        y_taken, moe_ready = sem("y_taken"), sem("moe_ready")
        dve_step = sem("dve_step")

        READERS = {"qk_w": "A", "woT": "A", "vo_w": "A", "out_bias": "A", "xn1T": "A", "q": "A", "ctxT": "AD",
                   "probsT": "A", "probsT_split": "AD", "attn": "D", "xn2T": "AD", "logits": "D", "gates": "A",
                   "outT": "D"}

        def probs_slot(t, g):
            return ("probsT_split" if g < SPLIT_G else "probsT", t, g)

        slots = [("qk_w",), ("xn1T", 0), ("ctxT", 0, 0), ("q", 0)] + [("ctxT", 0, g) for g in range(1, NG)]
        slots += [("ctxT", 1, 0), ("ctxT", 1, 1), ("woT",), ("xn1T", 1), ("q", 1), ("vo_w",), ("ctxT", 1, 2), ("ctxT", 1, 3),
                  probs_slot(0, 0), probs_slot(0, 1), probs_slot(0, 2), ("out_bias",), probs_slot(0, 3)]
        for b in range(1, B + 1):
            slots += [probs_slot(2 * b - 1, g) for g in range(NG)]
            if b + 1 < B:
                slots += [("ctxT", b + 1, 0), ("ctxT", b + 1, 1)]
            if b >= 2:
                slots += [("attn", b - 2)]
            if b >= 3:
                slots += [("logits", b - 3)]
            if b < B:
                tile = [probs_slot(2 * b, g) for g in range(NG)]
                if b + 1 < B:
                    slots += tile[:2] + [("xn1T", b + 1)] + tile[2:] + [("q", b + 1), ("ctxT", b + 1, 2), ("ctxT", b + 1, 3)]
                else:
                    slots += tile
            if b >= 2:
                slots += [("xn2T", b - 2)]
        late = {2: [("logits", 2), ("attn", 3)], 3: [("gates", 0)], 5: [("xn2T", 3)], 7: [("logits", 3)],
                15: [("gates", 1)], 20: [("outT", 0), ("outT", 1)], UNITS: [("outT", 2), ("outT", 3)]}
        for u in sorted(late):
            slots += late[u]
        place = {s: n for n, s in enumerate(slots)}

        banks = []
        for n in range(len(slots)):
            usable = (0, 1, 2, 3) if n < place[probs_slot(1, 0)] else (0, 1, 3) if n < place[("xn2T", B - 2)] else (0, 1)
            banks.append(max(usable, key=lambda k: banks[::-1].index(k) if k in banks else len(slots) - k))

        def bank(s):
            return (transit + acc)[banks[place[s]]]

        def before(n):
            return max((m for m in range(n) if banks[m] == banks[n]), default=None)

        def takes(s, reader):
            return sum(reader in READERS[k[0]] for k in slots[:place[s] + 1])

        def lows(n):
            return sum((m in LOW_ON_DVE) == (n in LOW_ON_DVE) for m in range(n + 1))

        def takings(k, i=None):
            whole = k + k // E * (BPH - 1)
            return whole + 1 + ((BPH - 1 if k % E == E - 1 else 0) if i is None else i)

        BATCH_COLUMNS = [slice(i * S, (i + 1) * S) for i in range(BPH)]

        last_y = [acc[0][:, 0:S], bank(("outT", B - 1))[:, 0:S]]

        def pieces_beside(b):
            each = -(-3 * E // (B - 1))
            return range(each * (b - 1), min(each * b, 3 * E)) if b else ()

        def unit(n):
            half, e, c = n // (E * FC), n // FC % E, n % FC
            return half, e, c

        block = stack.enter_context(nc.Block())

        @block.sync
        def _(sp):
            xv = x.rearrange("b (p j) d -> p b j d", j=NJ)
            ov = out.rearrange("b (p j) d -> p b j d", j=NJ)
            xs = x_sb[:, :, :].rearrange("p (b j) d -> p b j d", j=NJ)
            ys = y_sb[:, :, :].rearrange("p (b j) d -> p b j d", j=NJ)

            def load_ctx(b):
                keys = ctx[b, 0:FULL * P, :].rearrange("(p c) d -> p c d", c=FULL)
                sp.dma_start(ctx_sb[:, b, 0:8, :], keys[:, 0:8, :]).then_inc(ctx_loaded[b][0], 16)
                sp.dma_start(ctx_sb[:, b, 8:FULL, :], keys[:, 8:FULL, :]).then_inc(ctx_loaded[b][1], 16)
                sp.dma_start(ctx_sb[0:TAIL, b, FULL, :], ctx[b, FULL * P:KC, :]).then_inc(ctx_loaded[b][1], 16)

            sp.dma_start(xs[:, 0], xv[:, 0]).then_inc(x0_loaded, 16)
            sp.dma_start(wq_sb[:, :], wq).then_inc(wqk_loaded, 16)
            sp.dma_start(wk_sb[:, :], wk).then_inc(wqk_loaded, 16)
            sp.dma_start(bq_sb[:, :], bq.rearrange("(p o) -> p o", o=1)).then_inc(wqk_loaded, 16)
            load_ctx(0)
            sp.dma_start(xs[:, 1:B], xv[:, 1:B]).then_inc(x_loaded, 16)
            load_ctx(1)
            sp.dma_start(wv_sb[:, :], wv).then_inc(wvo_loaded, 16)
            sp.dma_start(wo_sb[:, :], wo).then_inc(wvo_loaded, 16)
            sp.dma_start(bv_sb[:, :], bv.rearrange("(p o) -> p o", o=1)).then_inc(wvo_loaded, 16)
            sp.dma_start(bo_sb[:, :], bo.rearrange("(o d) -> o d", o=1)).then_inc(wvo_loaded, 16)
            sp.dma_start(rw_sb[:, :], rw).then_inc(small_loaded, 16)
            sp.dma_start(rb_sb[:, :], rb.rearrange("(o e) -> o e", o=1).broadcast_to([P, E])).then_inc(small_loaded, 16)
            load_ctx(2)
            load_ctx(3)
            for k in range(3 * E):
                e, which = k // 3, k % 3
                if k >= RAW:
                    sp.wait_ge(wl_ready, k - RAW + 1)
                src = (w1[e], w3[e], w2[e].rearrange("(c p) d -> p c d", p=P))[which]
                dst = w_raw[:, k % RAW, :]
                if which == 2:
                    dst = dst.rearrange("p (c d) -> p c d", d=D)
                sp.dma_start(dst, src).then_inc(raw_loaded[k % RAW], 16)
            for half in range(HALVES):
                sp.wait_ge(act_took, takes(("gates", half), "A"))
                sp.dma_start(gates_dram[half].rearrange("e t p -> (e t) p"), gatesT[:, half, :]).then_inc(gates_out, 16)
                sp.wait_ge(gates_out, 16 * (half + 1))
                rows = gates_dram[half].rearrange("(o e) t p -> o (e t p)", o=1).broadcast_to([P, E * HT])
                sp.dma_start(gate_rows[:, half].rearrange("p e t -> p (e t)"), rows).then_inc(rows_loaded[half], 16)
            for b in range(B):
                sp.wait_ge(dve_took, takes(("outT", b), "D"))
                sp.dma_start(ov[:, b], ys[:, b]).then_inc(stored, 16)
            sp.wait_ge(stored, 16 * B)

        @block.gpsimd
        def _(pool):
            def rstd_of(ln, var_sem, rstd_sem, count):
                pool.wait_ge(var_sem, count)
                nc.gpsimd.tensor_tensor(rstd[:, ln, :], var_eps[:, ln, :], neg_half[:, :], ALU.pow).then_inc(rstd_sem, 1)

            def weight_low(k):
                pool.wait_ge(wh_ready, k + 1)
                e, which = k // 3, k % 3
                nc.gpsimd.tensor_tensor(w_lo[:, e, which, :], w_raw[:, k % RAW, :],
                                        w_hi[:, e, which, :].bitcast(F32), ALU.subtract).then_inc(wl_ready, 1)

            def context_low(b):
                pool.wait_ge(ctx_high, b + 1)
                nc.gpsimd.tensor_tensor(ctx_lo[:, :, :], ctx_sb[:, b, 0:SPLIT_C, :], ctx_hi[:, :, :].bitcast(F32),
                                        ALU.subtract).then_inc(ctx_low, 1)

            def gate_exp(half):
                pool.wait_ge(shift_ready, half + 1)
                nc.gpsimd.tensor_tensor(ex[:, :, :].rearrange("p t e -> p (t e)"), euler[:, :],
                                        shifted[:, :, :].rearrange("p t e -> p (t e)"), ALU.pow).then_inc(ex_ready, 1)

            def bias_x():
                pool.wait_ge(act_took, takes(("out_bias",), "A"))
                pool.wait_ge(x0_loaded, 16)
                pool.wait_ge(x_loaded, 16)
                nc.gpsimd.tensor_tensor(x_bias[:, :, :], x_sb[:, :, :],
                                        out_bias[:, :].rearrange("p (o d) -> p o d", o=1).broadcast_to([P, NT, D]),
                                        ALU.add).then_inc(xbias_ready, 1)

            nc.gpsimd.memset(ident[:, :], 0.0).then_inc(pool_step, 1)
            nc.gpsimd.memset(neg_half[:, :], -0.5).then_inc(pool_step, 1)
            nc.gpsimd.memset(below[:, :, :], 0.0).then_inc(pool_step, 1)
            pool.wait_ge(pool_step, 3)
            nc.gpsimd.affine_select(out=ident[:, :], in_=ident[:, :], compare_op=ALU.not_equal, fill=1.0, base=0,
                                    pattern=[[-1, P]], channel_multiplier=1).then_inc(consts_ready, 1)
            rstd_of(0, var1_ready, rstd1_ready, 1)
            nc.gpsimd.memset(ones_row[:, :], 1.0).then_inc(consts_ready, 1)
            nc.gpsimd.affine_select(out=below[:, :, :], in_=below[:, :, :], compare_op=ALU.is_ge, fill=1.0, base=0,
                                    pattern=[[-1, E], [1, E]], channel_multiplier=0).then_inc(consts_ready, 1)
            nc.gpsimd.memset(euler[:, :], 2.718281828459045).then_inc(pool_step, 1)
            rstd_of(0, var1_ready, rstd1_ready, 2)
            rstd_of(0, var1_ready, rstd1_ready, 3)
            context_low(0)
            bias_x()
            for b in range(1, B):
                if b >= 2:
                    rstd_of(1, var2_ready, rstd2_ready, b - 1)
                if b + 2 < B:
                    rstd_of(0, var1_ready, rstd1_ready, b + 3)
                pieces = list(pieces_beside(b))
                for k in pieces[:2]:
                    weight_low(k)
                context_low(b)
                for k in pieces[2:]:
                    weight_low(k)

            def low(n):
                pool.wait_ge(hh_done, n + 1)
                if n >= 3:
                    pool.wait_ge(y_done, n - 2)
                nc.gpsimd.tensor_tensor(h_lo[:, n % 3, :], h_f[n % 3], h_hi[:, n % 3, :].bitcast(F32),
                                        ALU.subtract).then_inc(hl_done, 1)

            low(0)
            rstd_of(1, var2_ready, rstd2_ready, B - 1)
            low(1)
            pool.wait_ge(pool_step, 4)
            gate_exp(0)
            for n in range(2, UNITS):
                if n == 3:
                    rstd_of(1, var2_ready, rstd2_ready, B)
                if n == 11:
                    gate_exp(1)
                if n not in LOW_ON_DVE:
                    low(n)

        @block.scalar
        def _(act):
            def take(s):
                act.wait_ge(filled, place[s] + 1)

            def copy(dst, src, s):
                nc.scalar.activation(dst, src, ACT.Copy).then_inc(act_took, 1)

            def take_xn1T(b):
                s = ("xn1T", b)
                take(s)
                copy(xn1T[:, :], bank(s)[:, 0:S], s)

            def take_q(b):
                s = ("q", b)
                take(s)
                if b >= 1:
                    act.wait_ge(q_split, b)
                nc.scalar.activation(q_f[:, :], bank(s)[:, 0:S], ACT.Identity, bias=q_bias[:, 0:1], scale=SCALE)
                nc.scalar.activation(q_hi[:, b % 2, :], bank(s)[:, 0:S], ACT.Identity, bias=q_bias[:, 0:1],
                                     scale=SCALE).then_inc(act_took, 1)

            def take_ctxT(b, g):
                s = ("ctxT", b, g)
                take(s)
                lo, hi = 4 * g * P, min(4 * (g + 1) * P, KC)
                copy(ctxT_hi[:, b % 2, lo:hi], bank(s)[:, 0:hi - lo], s)

            def take_probsT(t, g):
                s = probs_slot(t, g)
                take(s)
                b, j = t // NJ, t % NJ
                n, rows = len(group_chunks(g)), chunk_rows(4 * g)
                dst, c = (probsT_hi, 4 * g) if g < SPLIT_G else (probsT, 4 * g - SPLIT_C)
                copy(dst[0:rows, b % 2, c:c + n, j * P:(j + 1) * P],
                     bank(s)[0:rows, 0:n * P].rearrange("p (c q) -> p c q", q=P), s)

            def exp_half(t, h):
                if h == 0:
                    act.wait_ge(max_ready, t + 1)
                    if t >= 2:
                        act.wait_ge(filled, place[probs_slot(t - 2, NG - 1)] + 1)
                lo, hi = ((0, SPLIT_A), (SPLIT_A, KC))[h]
                nc.scalar.activation(probs[:, t % 2, lo:hi], scores[:, lo:hi], ACT.Exp, bias=neg_max[:, t:t + 1],
                                     accum_out=exp_sum[:, t, h:h + 1]).then_inc(exped, 1)

            def exps(t):
                exp_half(t, 0)
                exp_half(t, 1)

            def take_pc(b):
                act.wait_ge(pv_done, b + 1)
                if b >= 1:
                    act.wait_ge(filled, place[("attn", b - 1)] + 1)
                nc.scalar.activation(pcT[:, :], acc[0][:, 0:S], ACT.Copy).then_inc(pc_copied, 1)

            def take_xn2T(b):
                s = ("xn2T", b)
                take(s)
                copy(xn2T_hi[:, b * S:(b + 1) * S], bank(s)[:, 0:S], s)

            def take_gates(half):
                s = ("gates", half)
                take(s)
                copy(gatesT[:, half, :], bank(s)[0:TPH * E, 0:P], s)

            nc.scalar.preload_act_table(ACT.Exp)
            take(("qk_w",))
            qk = bank(("qk_w",))
            nc.scalar.activation(q_bias[:, :], qk[:, D:D + 1], ACT.Copy, scale=SCALE)
            nc.scalar.activation(qk_w[:, :], qk[:, 0:D], ACT.Copy).then_inc(act_took, 1)
            def take_weights(s, dst):
                take(s)
                copy(dst[:, :], bank(s)[:, 0:D], s)

            take_xn1T(0)
            take_ctxT(0, 0)
            take_q(0)
            for g in range(1, NG):
                take_ctxT(0, g)
            take_ctxT(1, 0)
            exp_half(0, 0)
            take_ctxT(1, 1)
            exp_half(0, 1)
            take_weights(("woT",), woT)
            take_xn1T(1)
            take_q(1)
            take_weights(("vo_w",), vo_w)
            exp_half(1, 0)
            take_ctxT(1, 2)
            take_ctxT(1, 3)
            exp_half(1, 1)
            take_probsT(0, 0)
            take_probsT(0, 1)
            take_probsT(0, 2)
            take_weights(("out_bias",), out_bias)
            take_probsT(0, 3)

            for b in range(1, B):
                for g in range(NG):
                    take_probsT(2 * b - 1, g)
                if b + 1 < B:
                    take_ctxT(b + 1, 0)
                    take_ctxT(b + 1, 1)
                exps(2 * b)
                for g in range(NG):
                    take_probsT(2 * b, g)
                    if g == 1 and b + 1 < B:
                        take_xn1T(b + 1)
                if b + 1 < B:
                    take_q(b + 1)
                    take_ctxT(b + 1, 2)
                else:
                    take_xn2T(b - 2)
                exp_half(2 * b + 1, 0)
                if b + 1 < B:
                    take_ctxT(b + 1, 3)
                exp_half(2 * b + 1, 1)
                if b + 1 < B and b >= 2:
                    take_xn2T(b - 2)
                take_pc(b - 1)

            def silu(n):
                act.wait_ge(a_done, n + 1)
                if n >= 2:
                    act.wait_ge(h_done, n - 1)
                nc.scalar.activation(act_a[:, n % 2, :], a_ps[n % 2], ACT.Silu).then_inc(silu_done, 1)

            def high(n):
                act.wait_ge(h_done, n + 1)
                if n >= 3:
                    act.wait_ge(y_done, n - 2)
                nc.scalar.activation(h_hi[:, n % 3, :], h_f[n % 3], ACT.Copy).then_inc(hh_done, 1)

            for g in range(NG):
                take_probsT(NT - 1, g)
            silu(0)
            silu(1)
            high(0)
            high(1)
            take_pc(B - 1)
            take_xn2T(B - 2)
            for n in range(2, UNITS - 1):
                silu(n)
                for s in late.get(n, ()):
                    if s[0] == "gates":
                        take_gates(s[1])
                    if s[0] == "xn2T":
                        take_xn2T(s[1])
                high(n)
            n = UNITS - 1
            act.wait_ge(a_done, UNITS)
            act.wait_ge(h_done, n - 1)
            for c in BATCH_COLUMNS:
                nc.scalar.activation(act_a[:, n % 2, c], a_ps[n % 2][:, c], ACT.Silu).then_inc(silu_done, 1)
            act.wait_ge(y_done, n - 2)
            for i, c in enumerate(BATCH_COLUMNS):
                act.wait_ge(h_done, UNITS + i)
                nc.scalar.activation(h_hi[:, n % 3, c], h_f[n % 3][:, c], ACT.Copy).then_inc(hh_done, 1)

        @block.vector
        def _(dve):
            steps = [0]

            def then(ins):
                steps[0] += 1
                ins.then_inc(dve_step, 1)
                dve.wait_ge(dve_step, steps[0])

            def norm_stats(ln, tiles, sem_out):
                for j in range(NJ):
                    nc.vector.bn_stats(stats[:, ln, j, :], tiles[:, j, :]).then_inc(dve_step, 1)
                steps[0] += NJ
                dve.wait_ge(dve_step, steps[0])
                for j in range(NJ):
                    nc.vector.bn_aggr(mean_var[:, ln, j, :], stats[:, ln, j, :]).then_inc(dve_step, 1)
                steps[0] += NJ
                dve.wait_ge(dve_step, steps[0])
                nc.vector.tensor_scalar(var_eps[:, ln, :], mean_var[:, ln, :, 1], EPS, None, ALU.add).then_inc(sem_out, 1)

            def normalise(ln, dst, tiles, sem_in, count, sem_out):
                dve.wait_ge(sem_in, count)
                for j in range(NJ):
                    nc.vector.tensor_scalar(dst[:, j, :], tiles[:, j, :], mean_var[:, ln, j, 0:1],
                                            rstd[:, ln, j:j + 1], ALU.subtract, ALU.mult).then_inc(sem_out, 1)

            def ln1_stats(b):
                dve.wait_ge(x0_loaded if b == 0 else x_loaded, 16)
                norm_stats(0, x_sb[:, NJ * b:NJ * (b + 1), :], var1_ready)

            def ln1(b):
                if b >= 1:
                    dve.wait_ge(filled, place[("xn1T", b - 1)] + 1)
                normalise(0, xn1, x_sb[:, NJ * b:NJ * (b + 1), :], rstd1_ready, b + 1, xn1_ready)

            def max_half(t, h):
                lo, hi = ((0, SPLIT_A), (SPLIT_A, KC))[h]
                dve.wait_ge(scored, 2 * t + h + 1)
                nc.vector.tensor_reduce(row_max[:, t, h:h + 1], scores[:, lo:hi], AXX, ALU.max).then_inc(dve_step, 1)
                steps[0] += 1
                if h == 1:
                    dve.wait_ge(dve_step, steps[0])
                    nc.vector.tensor_reduce(neg_max[:, t:t + 1], row_max[:, t, :], AXX, ALU.max,
                                            negate=True).then_inc(max_ready, 1)

            def maxima(t):
                max_half(t, 0)
                max_half(t, 1)

            def denominators(b):
                dve.wait_ge(exped, 4 * (b + 1))
                t = slice(NJ * b, NJ * (b + 1))
                then(nc.vector.tensor_tensor(denom[:, t], exp_sum[:, t, 0], exp_sum[:, t, 1], ALU.add))
                then(nc.vector.reciprocal(rdenom[:, t], denom[:, t]))

            def ctxT_low(b, g):
                s = ("ctxT", b, g)
                dve.wait_ge(act_took, takes(s, "A"))
                lo, hi = 4 * g * P, min(4 * (g + 1) * P, KC)
                nc.vector.tensor_tensor(ctxT_lo[:, b % 2, lo:hi], bank(s)[:, 0:hi - lo],
                                        ctxT_hi[:, b % 2, lo:hi].bitcast(F32), ALU.subtract).then_inc(dve_took, 1)

            def probs_low(t, g):
                s = probs_slot(t, g)
                dve.wait_ge(act_took, takes(s, "A"))
                b, j = t // NJ, t % NJ
                at = (slice(None), b % 2, slice(4 * g, 4 * g + 4), slice(j * P, (j + 1) * P))
                nc.vector.tensor_tensor(probsT_lo[at], bank(s)[:, 0:4 * P].rearrange("p (c q) -> p c q", q=P),
                                        probsT_hi[at].bitcast(F32), ALU.subtract).then_inc(dve_took, 1)

            def context_high(b):
                dve.wait_ge(ctx_loaded[b][0], 16)
                if b >= 1:
                    dve.wait_ge(pv_done, b)
                nc.vector.tensor_copy(ctx_hi[:, :, :], ctx_sb[:, b, 0:SPLIT_C, :]).then_inc(ctx_high, 1)

            def q_low(b):
                dve.wait_ge(act_took, takes(("q", b), "A"))
                nc.vector.tensor_tensor(q_lo[:, b % 2, :], q_f[:, :], q_hi[:, b % 2, :].bitcast(F32),
                                        ALU.subtract).then_inc(q_split, 1)

            def weight_high(k):
                e, which = k // 3, k % 3
                dve.wait_ge(raw_loaded[k % RAW], 16 * (k // RAW + 1))
                nc.vector.tensor_copy(w_hi[:, e, which, :], w_raw[:, k % RAW, :]).then_inc(wh_ready, 1)

            def residual(b):
                s = ("attn", b)
                if b == 0:
                    dve.wait_ge(xbias_ready, 1)
                denominators(b)
                dve.wait_ge(filled, place[s] + 1)
                for j in range(NJ):
                    t = NJ * b + j
                    ins = nc.vector.scalar_tensor_tensor(x2[:, t, :], bank(s)[:, j * P:(j + 1) * P], rdenom[:, t:t + 1],
                                                         x_bias[:, t, :], ALU.mult, ALU.add)
                    if j == NJ - 1:
                        ins.then_inc(dve_took, 1)
                dve.wait_ge(dve_took, takes(s, "D"))
                norm_stats(1, x2[:, NJ * b:NJ * (b + 1), :], var2_ready)

            def ln2(b):
                if b >= 1:
                    dve.wait_ge(filled, place[("xn2T", b - 1)] + 1)
                normalise(1, xn2, x2[:, NJ * b:NJ * (b + 1), :], rstd2_ready, b + 1, xn2_ready)

            def xn2T_low(b):
                s = ("xn2T", b)
                dve.wait_ge(act_took, takes(s, "A"))
                c = slice(b * S, (b + 1) * S)
                nc.vector.tensor_tensor(xn2T_lo[:, c], bank(s)[:, 0:S], xn2T_hi[:, c].bitcast(F32),
                                        ALU.subtract).then_inc(dve_took, 1)

            def take_logits(b):
                s = ("logits", b)
                dve.wait_ge(filled, place[s] + 1)
                nc.vector.tensor_tensor(logits[:, NJ * b:NJ * (b + 1), :],
                                        bank(s)[:, 0:NJ * E].rearrange("p (j e) -> p j e", e=E),
                                        rb_sb[:, :].rearrange("p (o e) -> p o e", o=1).broadcast_to([P, NJ, E]),
                                        ALU.add).then_inc(dve_took, 1)
                dve.wait_ge(dve_took, takes(s, "D"))

            def rank_experts(half):
                lg = logits[:, half * TPH:(half + 1) * TPH, :]
                as_j = lg.rearrange("p t (o j) -> p t o j", o=1).broadcast_to([P, TPH, E, E])
                as_e = lg.rearrange("p t (e o) -> p t e o", o=1).broadcast_to([P, TPH, E, E])
                then(nc.vector.tensor_reduce(top[:, :], lg, AXX, ALU.max))
                nc.vector.tensor_tensor(shifted[:, :, :], lg,
                                        top[:, :].rearrange("p (t o) -> p t o", o=1).broadcast_to([P, TPH, E]),
                                        ALU.subtract).then_inc(shift_ready, 1)
                nc.vector.tensor_tensor(greater[:, :, :, :], as_j, as_e, ALU.is_gt)
                then(nc.vector.tensor_tensor(equal[:, :, :, :], as_j, as_e, ALU.is_equal))
                then(nc.vector.tensor_tensor(equal[:, :, :, :], equal[:, :, :, :],
                                             below[:, :, :].rearrange("p (o e) j -> p o e j", o=1)
                                             .broadcast_to([P, TPH, E, E]), ALU.mult))
                then(nc.vector.tensor_tensor(beaten[:, :, :, :], greater[:, :, :, :], equal[:, :, :, :], ALU.add))
                then(nc.vector.tensor_reduce(rank[:, :, :], beaten[:, :, :, :], AXX, ALU.add))

            def make_gates(half):
                dve.wait_ge(ex_ready, half + 1)
                then(nc.vector.scalar_tensor_tensor(kept[:, :, :], rank[:, :, :], 1.5, ex[:, :, :], ALU.is_lt, ALU.mult))
                then(nc.vector.tensor_reduce(kept_sum[:, :], kept[:, :, :], AXX, ALU.add))
                then(nc.vector.reciprocal(rkept[:, :], kept_sum[:, :]))
                nc.vector.tensor_tensor(gates[:, :, :].rearrange("p e t -> p t e"), kept[:, :, :],
                                        rkept[:, :].rearrange("p (t o) -> p t o", o=1).broadcast_to([P, TPH, E]),
                                        ALU.mult).then_inc(gates_ready, 1)

            nc.vector.memset(probs[:, 0, 0:P], 0.0).then_inc(zeros_ready, 1)
            if KPAD > KC:
                nc.vector.memset(ctxT_hi[:, :, KC:KPAD].bitcast(F32), 0.0).then_inc(consts_ready, 1)
                nc.vector.memset(ctxT_lo[:, :, KC:KPAD].bitcast(F32), 0.0).then_inc(consts_ready, 1)
            ln1_stats(0)
            ln1(0)
            ctxT_low(0, 0)
            q_low(0)
            for g in range(1, NG):
                ctxT_low(0, g)
            maxima(0)
            ln1_stats(1)
            ctxT_low(1, 0)
            ln1(1)
            ctxT_low(1, 1)
            maxima(1)
            q_low(1)
            ln1_stats(2)
            context_high(0)
            ctxT_low(1, 2)
            ctxT_low(1, 3)
            for g in range(SPLIT_G):
                probs_low(0, g)

            for b in range(1, B):
                if b == 1:
                    max_half(2 * b, 0)
                for g in range(SPLIT_G):
                    probs_low(2 * b - 1, g)
                if b >= 2:
                    max_half(2 * b, 0)
                max_half(2 * b, 1)
                if b + 1 < B:
                    ln1(b + 1)
                    ctxT_low(b + 1, 0)
                    ctxT_low(b + 1, 1)
                if b == 1:
                    dve.wait_ge(small_loaded, 32)
                    then(nc.vector.tensor_copy(rw_hi[:, :], rw_sb[:, :]))
                    then(nc.vector.tensor_tensor(rw_lo[:, :], rw_sb[:, :], rw_hi[:, :].bitcast(F32), ALU.subtract))
                    dve.wait_ge(consts_ready, 5)
                if b >= 2:
                    residual(b - 2)
                if b >= 3:
                    take_logits(b - 3)
                for g in range(SPLIT_G):
                    probs_low(2 * b, g)
                if b == B - 1:
                    ln2(b - 2)
                maxima(2 * b + 1)
                if b == B - 1:
                    xn2T_low(b - 2)
                elif b >= 2:
                    ln2(b - 2)
                if b + 2 < B:
                    ln1_stats(b + 2)
                if b + 1 < B:
                    q_low(b + 1)
                    ctxT_low(b + 1, 2)
                    ctxT_low(b + 1, 3)
                for k in pieces_beside(b):
                    weight_high(k)
                if b + 1 < B and b >= 2:
                    xn2T_low(b - 2)
                context_high(b)

            def combine(k):
                half, e = k // E, k % E
                dve.wait_ge(y_done, FC * (k + 1))
                if e == 0:
                    dve.wait_ge(rows_loaded[half], 16)
                dst = moeT[:, :] if e == 0 else gated[:, k % 2, :]
                if e < E - 1:
                    nc.vector.tensor_tensor(dst, acc[(k + 1) % 2][:, 0:HT], gate_rows[:, half, e, :], ALU.mult).then_inc(y_taken, 1)
                    if e:
                        dve.wait_ge(y_taken, takings(k, 0))
                        then(nc.vector.tensor_tensor(moeT[:, :], moeT[:, :], dst, ALU.add))
                    return
                for i, c in enumerate(BATCH_COLUMNS):
                    src = acc[(k + 1) % 2][:, c]
                    if k == HALVES * E - 1:
                        dve.wait_ge(y_done, UNITS + i)
                        src = last_y[i]
                    nc.vector.tensor_tensor(dst[:, c], src, gate_rows[:, half, e, c], ALU.mult).then_inc(y_taken, 1)
                for i, c in enumerate(BATCH_COLUMNS):
                    dve.wait_ge(y_taken, takings(k, i))
                    nc.vector.tensor_tensor(moeT[:, c], moeT[:, c], dst[:, c], ALU.add).then_inc(moe_ready, 1)

            def finish(b):
                s = ("outT", b)
                dve.wait_ge(filled, place[s] + 1)
                t = slice(b * NJ, (b + 1) * NJ)
                nc.vector.tensor_tensor(y_sb[:, t, :], bank(s)[:, 0:S].rearrange("p (t d) -> p t d", d=D),
                                        x2[:, t, :], ALU.add).then_inc(dve_took, 1)

            def product(n):
                dve.wait_ge(silu_done, n + 1)
                dve.wait_ge(b_done, n + 1)
                if n >= 3:
                    dve.wait_ge(hl_dve if n - 3 in LOW_ON_DVE else hl_done, lows(n - 3))
                nc.vector.tensor_tensor(h_f[n % 3], b_ps[n % 2], act_a[:, n % 2, :], ALU.mult).then_inc(h_done, 1)

            def low(n):
                dve.wait_ge(hh_done, n + 1)
                dve.wait_ge(y_done, n - 2)
                nc.vector.tensor_tensor(h_lo[:, n % 3, :], h_f[n % 3], h_hi[:, n % 3, :].bitcast(F32),
                                        ALU.subtract).then_inc(hl_dve, 1)

            for g in range(SPLIT_G):
                probs_low(NT - 1, g)
            product(0)
            residual(B - 2)
            product(1)
            take_logits(1)
            rank_experts(0)
            ln2(B - 2)
            xn2T_low(B - 2)
            make_gates(0)
            for n in range(2, UNITS - 1):
                product(n)
                if n in LOW_ON_DVE:
                    low(n)
                if n == 2:
                    take_logits(2)
                    residual(3)
                if n == 3:
                    ln2(3)
                if n == 6:
                    xn2T_low(3)
                if n == 8:
                    take_logits(3)
                    rank_experts(1)
                if n == 13:
                    make_gates(1)
                if n >= 6 and n % FC == 2 and n != UNITS - 2:
                    combine((n - 6) // FC)
                if n == UNITS - 3:
                    combine(HALVES * E - 2)
                if n == 21:
                    finish(0)
                    finish(1)
            n = UNITS - 1
            dve.wait_ge(b_done, UNITS)
            dve.wait_ge(hl_dve if n - 3 in LOW_ON_DVE else hl_done, lows(n - 3))
            for i, c in enumerate(BATCH_COLUMNS):
                dve.wait_ge(silu_done, UNITS + i)
                nc.vector.tensor_tensor(h_f[n % 3][:, c], b_ps[n % 2][:, c], act_a[:, n % 2, c], ALU.mult).then_inc(h_done, 1)
            dve.wait_ge(y_done, n - 2)
            for i, c in enumerate(BATCH_COLUMNS):
                dve.wait_ge(hh_done, UNITS + i)
                nc.vector.tensor_tensor(h_lo[:, n % 3, c], h_f[n % 3][:, c], h_hi[:, n % 3, c].bitcast(F32),
                                        ALU.subtract).then_inc(hl_dve, 1)
            combine(HALVES * E - 1)
            finish(2)
            finish(3)

        @block.tensor
        def _(pe):
            def open_slot(s):
                n = before(place[s])
                if n is not None:
                    emptied(slots[n])

            def emptied(old):
                if READERS[old[0]].endswith("D"):
                    pe.wait_ge(dve_took, takes(old, "D"))
                else:
                    pe.wait_ge(act_took, takes(old, "A"))

            def last_in(i):
                return slots[max(n for n in range(len(slots)) if banks[n] == i)]

            def matmul3(dst, lhs_hi, lhs_lo, rhs_hi, rhs_lo, first=True, last=True):
                nc.tensor.matmul(dst, lhs_hi, rhs_hi, start=first, stop=False)
                nc.tensor.matmul(dst, lhs_hi, rhs_lo, start=False, stop=False)
                return nc.tensor.matmul(dst, lhs_lo, rhs_hi, start=False, stop=last)

            def fill_xn1T(b):
                s = ("xn1T", b)
                open_slot(s)
                pe.wait_ge(xn1_ready, NJ * (b + 1))
                for j in range(NJ):
                    ins = nc.tensor.transpose(bank(s)[:, j * P:(j + 1) * P], xn1[:, j, :], ident[:, :])
                ins.then_inc(filled, 1)

            def fill_q(b):
                s = ("q", b)
                open_slot(s)
                pe.wait_ge(act_took, takes(("xn1T", b), "A"))
                nc.tensor.matmul(bank(s)[:, 0:S], qk_w[:, :], xn1T[:, :], start=True, stop=True).then_inc(filled, 1)

            def fill_ctxT(b, g):
                s = ("ctxT", b, g)
                open_slot(s)
                if g in (0, 2):
                    pe.wait_ge(ctx_loaded[b][g // 2], (16, 32)[g // 2])
                for i, c in enumerate(group_chunks(g)):
                    r = chunk_rows(c)
                    ins = nc.tensor.transpose(bank(s)[:, i * P:i * P + r], ctx_sb[0:r, b, c, :], ident[0:r, 0:r])
                ins.then_inc(filled, 1)

            def fill_probsT(t, g):
                s = probs_slot(t, g)
                open_slot(s)
                pe.wait_ge(exped, 2 * t + (1 if 4 * (g + 1) * P <= SPLIT_A else 2))
                for i, c in enumerate(group_chunks(g)):
                    r = chunk_rows(c)
                    ins = nc.tensor.transpose(bank(s)[0:r, i * P:(i + 1) * P],
                                              probs[:, t % 2, c * P:c * P + r], ident[:, :])
                ins.then_inc(filled, 1)

            def score(t, h):
                b, j = t // NJ, t % NJ
                if j == 0:
                    pe.wait_ge(q_split, b + 1)
                if t >= 1:
                    pe.wait_ge(exped, 2 * t - 1 + h)
                lo, end = (0, SPLIT_A) if h == 0 else (SPLIT_A, KPAD)
                q = slice(j * P, (j + 1) * P)
                pieces = [(c, min(c + BANK, end)) for c in range(lo, end, BANK)]
                hi, low = q_hi[:, b % 2, q], q_lo[:, b % 2, q]
                for c0, c1 in pieces:
                    if j == 0:
                        pe.wait_ge(dve_took, takes(("ctxT", b, c0 // BANK), "D"))
                    nc.tensor.matmul(scores[:, c0:c1], hi, ctxT_hi[:, b % 2, c0:c1], start=True, stop=False)
                    nc.tensor.matmul(scores[:, c0:c1], hi, ctxT_lo[:, b % 2, c0:c1], start=False, stop=False)
                for c0, c1 in pieces:
                    ins = nc.tensor.matmul(scores[:, c0:c1], low, ctxT_hi[:, b % 2, c0:c1], start=False, stop=True)
                ins.then_inc(scored, 1)

            VALUE_ORDER = [*range(SPLIT_C, NCH), *range(SPLIT_C)]

            def values(b, first, end):
                if first == 0:
                    pe.wait_ge(act_took, takes(probs_slot(NJ * b + 1, NG - 1), "A"))
                    if b >= 1:
                        pe.wait_ge(pc_copied, b)
                    else:
                        emptied(last_in(2))
                for n in range(first, end):
                    c = VALUE_ORDER[n]
                    if c == 0:
                        pe.wait_ge(dve_took, takes(probs_slot(NJ * b + 1, SPLIT_G - 1), "D"))
                        pe.wait_ge(ctx_low, b + 1)
                    if c < SPLIT_C:
                        ins = matmul3(acc[0][:, 0:S], ctx_hi[:, c, :], ctx_lo[:, c, :], probsT_hi[:, b % 2, c, :],
                                      probsT_lo[:, b % 2, c, :], first=(n == 0), last=(n == NCH - 1))
                    else:
                        r = chunk_rows(c)
                        ins = nc.tensor.matmul(acc[0][:, 0:S], ctx_sb[0:r, b, c, :], probsT[0:r, b % 2, c - SPLIT_C, :],
                                               start=(n == 0), stop=(n == NCH - 1))
                if end == NCH:
                    ins.then_inc(pv_done, 1)

            def fill_attn(b):
                s = ("attn", b)
                open_slot(s)
                pe.wait_ge(pc_copied, b + 1)
                for j in range(NJ):
                    ins = nc.tensor.matmul(bank(s)[:, j * P:(j + 1) * P], pcT[:, j * P:(j + 1) * P], vo_w[:, :],
                                           start=True, stop=True)
                ins.then_inc(filled, 1)

            def fill_xn2T(b):
                s = ("xn2T", b)
                open_slot(s)
                pe.wait_ge(xn2_ready, NJ * (b + 1))
                for j in range(NJ):
                    ins = nc.tensor.transpose(bank(s)[:, j * P:(j + 1) * P], xn2[:, j, :], ident[:, :])
                ins.then_inc(filled, 1)

            def fill_logits(b):
                s = ("logits", b)
                open_slot(s)
                pe.wait_ge(dve_took, takes(("xn2T", b), "D"))
                for j in range(NJ):
                    q = slice(b * S + j * P, b * S + (j + 1) * P)
                    ins = matmul3(bank(s)[:, j * E:(j + 1) * E], xn2T_hi[:, q], xn2T_lo[:, q], rw_hi[:, :], rw_lo[:, :])
                ins.then_inc(filled, 1)

            def fill_gates(half):
                s = ("gates", half)
                open_slot(s)
                pe.wait_ge(gates_ready, half + 1)
                nc.tensor.transpose(bank(s)[0:TPH * E, 0:P], gates[:, :, :].rearrange("p e t -> p (e t)"),
                                    ident[:, :]).then_inc(filled, 1)

            def fill_outT(b):
                s = ("outT", b)
                open_slot(s)
                pe.wait_ge(moe_ready, b + 1)
                for j in range(NJ):
                    c = b % BPH * S + j * P
                    ins = nc.tensor.transpose(bank(s)[:, j * P:(j + 1) * P], moeT[:, c:c + P], ident[:, :])
                ins.then_inc(filled, 1)

            FILL = {"logits": fill_logits, "attn": fill_attn, "gates": fill_gates, "xn2T": fill_xn2T, "outT": fill_outT}

            def fill_product(s, *pairs):
                open_slot(s)
                for i, (lhsT, rhs) in enumerate(pairs):
                    ins = nc.tensor.matmul(bank(s)[:, 0:D], lhsT, rhs, start=(i == 0), stop=(i == len(pairs) - 1))
                ins.then_inc(filled, 1)

            pe.wait_ge(zeros_ready, 1)
            for _ in range(WARM):
                nc.tensor.matmul(acc[1][:, 0:P], probs[:, 0, 0:P], probs[:, 0, 0:P], start=True, stop=True)
            pe.wait_ge(wqk_loaded, 48)
            qk = bank(("qk_w",))
            nc.tensor.matmul(qk[:, 0:D], wq_sb[:, :], wk_sb[:, :], start=True, stop=True)
            nc.tensor.matmul(qk[:, D:D + 1], wk_sb[:, :], bq_sb[:, :], start=True, stop=True).then_inc(filled, 1)
            pe.wait_ge(consts_ready, 1)
            fill_xn1T(0)
            fill_ctxT(0, 0)
            fill_q(0)
            for g in range(1, NG):
                fill_ctxT(0, g)

            def fill_woT():
                pe.wait_ge(wvo_loaded, 64)
                open_slot(("woT",))
                nc.tensor.transpose(bank(("woT",))[:, 0:D], wo_sb[:, :], ident[:, :]).then_inc(filled, 1)

            def expert_a(n):
                half, e, c = unit(n)
                tok = slice(half * HT, (half + 1) * HT)
                f = slice(c * P, (c + 1) * P)
                if n % FC == 0 and half == 0:
                    pe.wait_ge(wl_ready, 3 * (e + 1))
                if n % (E * FC) == 0:
                    pe.wait_ge(dve_took, takes(("xn2T", BPH * (half + 1) - 1), "D"))
                if n >= 2:
                    pe.wait_ge(silu_done, n - 1)
                else:
                    pe.wait_ge(exped, 2 * NT - 1)
                matmul3(a_ps[n % 2], w_hi[:, e, 0, f], w_lo[:, e, 0, f], xn2T_hi[:, tok], xn2T_lo[:, tok]).then_inc(a_done, 1)

            def expert_b(n):
                half, e, c = unit(n)
                tok = slice(half * HT, (half + 1) * HT)
                f = slice(c * P, (c + 1) * P)
                if n >= 2:
                    pe.wait_ge(h_done, n - 1)
                else:
                    pe.wait_ge(exped, 2 * NT)
                matmul3(b_ps[n % 2], w_hi[:, e, 1, f], w_lo[:, e, 1, f], xn2T_hi[:, tok], xn2T_lo[:, tok]).then_inc(b_done, 1)

            def expert_out(n):
                half, e, c = unit(n)
                k = n // FC
                if c == 0 and k >= 2:
                    pe.wait_ge(y_taken, takings(k - 2))
                if c == 0 and k == 0:
                    emptied(last_in(3))
                if c == 0 and k == 1:
                    pe.wait_ge(pc_copied, B)
                pe.wait_ge(hl_dve if n in LOW_ON_DVE else hl_done, lows(n))
                d = slice(c * D, (c + 1) * D)
                matmul3(acc[(k + 1) % 2][:, 0:HT], w_hi[:, e, 2, d], w_lo[:, e, 2, d], h_hi[:, n % 3, :], h_lo[:, n % 3, :],
                        first=(c == 0), last=(c == FC - 1)).then_inc(y_done, 1)

            def last_expert_out(n):
                k, ch = n // FC, n % FC
                if ch == 0:
                    pe.wait_ge(y_taken, takings(k - 2))
                    emptied(slots[before(place[("outT", B - 1)])])
                d = slice(ch * D, (ch + 1) * D)
                w2_hi, w2_lo = w_hi[:, E - 1, 2, d], w_lo[:, E - 1, 2, d]
                last = n == UNITS - 1
                for i, c in enumerate(BATCH_COLUMNS):
                    dst, h_high = last_y[i], h_hi[:, n % 3, c]
                    pe.wait_ge(hh_done, n + 1 + (i if last else 0))
                    nc.tensor.matmul(dst, w2_lo, h_high, start=(ch == 0), stop=False)
                    nc.tensor.matmul(dst, w2_hi, h_high, start=False, stop=False)
                    pe.wait_ge(hl_dve if n in LOW_ON_DVE else hl_done, lows(n) + (i if last else 0))
                    ins = nc.tensor.matmul(dst, w2_hi, h_lo[:, n % 3, c], start=False, stop=last)
                    if last or i == BPH - 1:
                        ins.then_inc(y_done, 1)

            def value_run(b, *cuts):
                if b >= 0:
                    values(b, *cuts)

            score(0, 0)
            score(0, 1)
            fill_ctxT(1, 0)
            fill_ctxT(1, 1)
            fill_woT()
            score(1, 0)
            fill_xn1T(1)
            score(1, 1)
            fill_q(1)
            pe.wait_ge(act_took, takes(("woT",), "A"))
            fill_product(("vo_w",), (wv_sb[:, :], woT[:, :]))
            fill_ctxT(1, 2)
            fill_ctxT(1, 3)
            fill_probsT(0, 0)
            score(2, 0)
            fill_probsT(0, 1)
            fill_probsT(0, 2)
            pe.wait_ge(consts_ready, 5)
            fill_product(("out_bias",), (bv_sb[:, 0:1].broadcast_to([P, P]), woT[:, :]), (ones_row[:, :], bo_sb[:, :]))
            fill_probsT(0, 3)

            for b in range(1, B):
                v = b - 1
                nxt = b + 1 < B
                fill_probsT(2 * b - 1, 0)
                fill_probsT(2 * b - 1, 1)
                if b >= 2:
                    score(2 * b, 0)
                fill_probsT(2 * b - 1, 2)
                if b == 1:
                    score(2 * b, 1)
                fill_probsT(2 * b - 1, 3)
                if b >= 2:
                    score(2 * b, 1)
                if nxt:
                    fill_ctxT(b + 1, 0)
                value_run(v, 0, 1)
                if nxt:
                    fill_ctxT(b + 1, 1)
                value_run(v, 1, 4)
                if b >= 2:
                    fill_attn(b - 2)
                value_run(v, 4, 5)
                if b >= 3:
                    fill_logits(b - 3)
                value_run(v, 5, 6)
                fill_probsT(2 * b, 0)
                fill_probsT(2 * b, 1)
                if nxt:
                    fill_xn1T(b + 1)
                score(2 * b + 1, 0)
                fill_probsT(2 * b, 2)
                fill_probsT(2 * b, 3)
                if nxt:
                    fill_q(b + 1)
                score(2 * b + 1, 1)
                if not nxt:
                    fill_xn2T(b - 2)
                value_run(v, 6, 7)
                if nxt:
                    fill_ctxT(b + 1, 2)
                value_run(v, 7, 10)
                if nxt:
                    fill_ctxT(b + 1, 3)
                value_run(v, 10, 12)
                if nxt and b >= 2:
                    fill_xn2T(b - 2)
                value_run(v, 12, 13)

            fill_probsT(NT - 1, 0)
            fill_probsT(NT - 1, 1)
            expert_a(0)
            fill_probsT(NT - 1, 2)
            fill_probsT(NT - 1, 3)
            expert_b(0)
            fill_attn(B - 2)
            expert_a(1)
            fill_logits(B - 3)
            expert_b(1)
            values(B - 1, 0, NCH)
            fill_xn2T(B - 2)
            expert_out(0)
            for n in range(2, UNITS):
                expert_a(n)
                expert_b(n)
                if n >= 3:
                    (expert_out if n - 2 < UNITS - FC else last_expert_out)(n - 2)
                for s in late.get(n, ()):
                    FILL[s[0]](*s[1:])
            last_expert_out(UNITS - 2)
            last_expert_out(UNITS - 1)
            for s in late[UNITS]:
                FILL[s[0]](*s[1:])


_INS = ["x", "ctx_1024", "L0_xattn_Wk", "L0_xattn_Wv", "L0_xattn_bv", "L0_xattn_Wq", "L0_xattn_bq", "L0_xattn_Wo",
        "L0_xattn_bo", "L0_ffn_router_w", "L0_ffn_router_b", "L0_ffn_w1", "L0_ffn_w3", "L0_ffn_w2"]


def kernel(**inputs):
    import numpy as np
    import concourse.bacc as bacc
    from concourse import mybir as mb
    from concourse.bass_utils import run_bass_kernel_spmd as run

    nc = bacc.Bacc("TRN2", target_bir_lowering=False, num_devices=1)
    arrays, args = {}, []
    for name in _INS:
        a = np.ascontiguousarray(inputs[name])
        arrays[f"in_{name}_dram"] = a
        args.append(nc.dram_tensor(f"in_{name}_dram", a.shape, mb.dt.from_np(a.dtype), kind="ExternalInput").ap())
    shape = inputs["x"].shape
    out = nc.dram_tensor("out_dram", shape, mb.dt.float32, kind="ExternalOutput").ap()
    xattn_moe_program(nc, *args, out)
    r = run(nc, [arrays], core_ids=[0])
    return r.results[0]["out_dram"]
```
